# Optimizing a Trainium2 kernel written in Bass

```python
import numpy as np
import jax
import jax.numpy as jnp

def _softmax(x, axis=-1):
    return jax.nn.softmax(x, axis=axis)

def _gelu(x):
    return jax.nn.gelu(x, approximate=True)

def _silu(x):
    return jax.nn.silu(x)

def _sigmoid(x):
    return jax.nn.sigmoid(x)

def _layernorm(x, axis=-1, eps=1e-05):
    m = jnp.mean(x, axis=axis, keepdims=True)
    v = jnp.var(x, axis=axis, keepdims=True)
    return (x - m) / jnp.sqrt(v + eps)

def _scatter_add(tgt, idx, src, axis=0):
    return tgt.at[idx].add(src)

def _segment_sum(src, seg, n):
    return jax.ops.segment_sum(src, seg, n)
kernel_name = 'mk_macaron_d1_jaxref_r2_e80290'

def setup_inputs(seed: int=0):
    np.random.seed(seed)
    _w = jnp.asarray

    def _L0_attn_setup():
        import jax, jax.numpy as jnp
        import numpy as np
        N_HEAD = 16
        EPS = 1e-06

        def _linear_attention(q, k, v):
            B, H, D = (q.shape[1], q.shape[2], q.shape[3])

            def step(carry, qkv_t):
                S, z = carry
                qt, kt, vt = qkv_t
                S = S + kt[..., :, None] * vt[..., None, :]
                z = z + kt
                num = jnp.einsum('bhi,bhij->bhj', qt, S)
                den = jnp.sum(qt * z, axis=-1, keepdims=True)
                return ((S, z), num / (den + EPS))
            S0 = jnp.zeros((B, H, D, D), q.dtype)
            z0 = jnp.zeros((B, H, D), q.dtype)
            _, y = jax.lax.scan(step, (S0, z0), (q, k, v))
            return y
        key = jax.random.key(seed)
        k1, k2, k3 = jax.random.split(key, 3)
        B, T, C = (2, 1024, 512)
        x = jax.random.normal(k1, (B, T, C), dtype=jnp.float32)
        w_attn = jax.random.normal(k2, (C, 3 * C), dtype=jnp.float32) * 0.02
        w_proj = jax.random.normal(k3, (C, C), dtype=jnp.float32) * 0.02
        return {'x': x, 'w_attn': w_attn, 'w_proj': w_proj}
    _L0_attn_in = _L0_attn_setup()

    def _L0_ffn_setup():
        import jax, jax.numpy as jnp
        import numpy as np
        D_MODEL = 512
        M = 64
        INNER = 16
        key = jax.random.key(seed)
        ks = jax.random.split(key, 9)

        def init(k, shape, fan_in):
            bound = 1.0 / np.sqrt(fan_in)
            return jax.random.uniform(k, shape, jnp.float32, -bound, bound)
        x = jax.random.normal(ks[0], (16, 2048, D_MODEL), dtype=jnp.float32)
        Win = init(ks[1], (D_MODEL, M), D_MODEL)
        bin_ = init(ks[2], (M,), D_MODEL)
        W1 = init(ks[3], (M, INNER), 1)
        b1 = init(ks[4], (M, INNER), 1)
        W2 = init(ks[5], (M, INNER), INNER)
        b2 = init(ks[6], (M,), INNER)
        Wout = init(ks[7], (M, D_MODEL), M)
        bout = init(ks[8], (D_MODEL,), M)
        return {'x': x, 'Win': Win, 'bin_': bin_, 'W1': W1, 'b1': b1, 'W2': W2, 'b2': b2, 'Wout': Wout, 'bout': bout}
    _L0_ffn_in = _L0_ffn_setup()
    _d = {'L0_attn_x': _L0_attn_in['x'], 'L0_attn_w_attn': _L0_attn_in['w_attn'], 'L0_attn_w_proj': _L0_attn_in['w_proj'], 'L0_ffn_Win': _L0_ffn_in['Win'], 'L0_ffn_bin_': _L0_ffn_in['bin_'], 'L0_ffn_W1': _L0_ffn_in['W1'], 'L0_ffn_b1': _L0_ffn_in['b1'], 'L0_ffn_W2': _L0_ffn_in['W2'], 'L0_ffn_b2': _L0_ffn_in['b2'], 'L0_ffn_Wout': _L0_ffn_in['Wout'], 'L0_ffn_bout': _L0_ffn_in['bout']}
    _x0 = _d['L0_attn_x']
    _d['L0_attn_x'] = jax.random.normal(jax.random.fold_in(jax.random.key(seed), 1), (16, 1024, 512), dtype=_x0.dtype)
    del _x0
    return _d

def reference(L0_attn_x, L0_attn_w_attn, L0_attn_w_proj, L0_ffn_Win, L0_ffn_bin_, L0_ffn_W1, L0_ffn_b1, L0_ffn_W2, L0_ffn_b2, L0_ffn_Wout, L0_ffn_bout):

    def _L0_attn_ref(x, w_attn, w_proj):
        import jax, jax.numpy as jnp
        import numpy as np
        N_HEAD = 16
        EPS = 1e-06

        def _linear_attention(q, k, v):
            B, H, D = (q.shape[1], q.shape[2], q.shape[3])

            def step(carry, qkv_t):
                S, z = carry
                qt, kt, vt = qkv_t
                S = S + kt[..., :, None] * vt[..., None, :]
                z = z + kt
                num = jnp.einsum('bhi,bhij->bhj', qt, S)
                den = jnp.sum(qt * z, axis=-1, keepdims=True)
                return ((S, z), num / (den + EPS))
            S0 = jnp.zeros((B, H, D, D), q.dtype)
            z0 = jnp.zeros((B, H, D), q.dtype)
            _, y = jax.lax.scan(step, (S0, z0), (q, k, v))
            return y
        B, T, C = x.shape
        H = N_HEAD
        D = C // H
        qkv = x @ w_attn
        q, k, v = jnp.split(qkv, 3, axis=-1)

        def to_tbhd(a):
            return a.reshape(B, T, H, D).transpose(1, 0, 2, 3)
        q = jax.nn.elu(to_tbhd(q)) + 1.0
        k = jax.nn.elu(to_tbhd(k)) + 1.0
        v = to_tbhd(v)
        y = _linear_attention(q, k, v)
        y = y.transpose(1, 0, 2, 3).reshape(B, T, C)
        return y @ w_proj

    def _L0_ffn_ref(x, Win, bin_, W1, b1, W2, b2, Wout, bout):
        import jax, jax.numpy as jnp
        import numpy as np
        D_MODEL = 512
        M = 64
        INNER = 16
        s = jnp.einsum('btd,dm->btm', x, Win) + bin_
        h = jax.nn.relu(s[..., None] * W1 + b1)
        g = jnp.einsum('btmh,mh->btm', h, W2) + b2
        out = jnp.einsum('btm,md->btd', g, Wout) + bout
        return out
    x = L0_attn_x
    x = x + 0.5 * _L0_ffn_ref(_layernorm(x, axis=-1), L0_ffn_Win, L0_ffn_bin_, L0_ffn_W1, L0_ffn_b1, L0_ffn_W2, L0_ffn_b2, L0_ffn_Wout, L0_ffn_bout)
    x = x + _L0_attn_ref(_layernorm(x, axis=-1), L0_attn_w_attn, L0_attn_w_proj)
    x = x + 0.5 * _L0_ffn_ref(_layernorm(x, axis=-1), L0_ffn_Win, L0_ffn_bin_, L0_ffn_W1, L0_ffn_b1, L0_ffn_W2, L0_ffn_b2, L0_ffn_Wout, L0_ffn_bout)
    return x

_drawn_inputs = setup_inputs


def setup_inputs(seed=0):
    import zlib

    import numpy as np

    out = dict(_drawn_inputs(seed))
    spreads = {}
    factors = {'L0_ffn_bin_': 8.0}
    for name, (base, spread) in spreads.items():
        noise = np.random.default_rng([zlib.crc32(name.encode()), seed]).standard_normal(out[name].shape)
        drawn = base * np.exp(spread * noise) if base else spread * noise
        out[name] = jnp.asarray(drawn.astype(out[name].dtype))
    for name, factor in factors.items():
        out[name] = (out[name] * factor).astype(out[name].dtype)
    return out
```

```python
from contextlib import ExitStack

import concourse.bass as bass
from concourse import mybir

F32 = mybir.dt.float32
F32R = mybir.dt.float32r
ALU = mybir.AluOpType
ACT = mybir.ActivationFunctionType

P = 128
TILES = 4
BLK = P * TILES
SLOTS = 4


class Queue:

    def __init__(self, sem):
        self.sem, self.count, self.ops, self.seen = sem, 0, [], {}

    def wait(self, *marks):
        for mark in marks:
            if mark is None:
                continue
            sem, value = mark
            if self.seen.get(id(sem), 0) < value:
                self.seen[id(sem)] = value
                self.ops.append(lambda e, sem=sem, value=value: e.wait_ge(sem, value))

    def put(self, fn):
        self.ops.append(fn)

    def do(self, fn):
        self.count += 1
        sem = self.sem
        self.ops.append(lambda e: fn(e).then_inc(sem, 1))
        return sem, self.count

    def dma(self, fn, sem, total):
        self.ops.append(lambda e: fn(e).then_inc(sem, 16))
        return sem, total

    def run(self, eng):
        for op in self.ops:
            op(eng)


def macaron_kernel(nc, x, w_attn, w_proj, Win, bin_, W1, b1, W2, b2, Wout, bout, out):
    B, T, C = x.shape
    M, INNER = W1.shape
    D = 32
    KC = C // P
    NB = B * T // BLK
    PER = T // BLK
    HI = INNER // 2
    LN_EPS, EPS = 1e-5, 1e-6
    assert C == 512 and M == 64 and INNER == 16 and T % BLK == 0

    xv = x.rearrange("b t c -> (b t) c").rearrange("(k q p) c -> k p q c", q=TILES, p=P)
    ov = out.rearrange("b t c -> (b t) c").rearrange("(k q p) c -> k p q c", q=TILES, p=P)

    ctx = ExitStack()
    with ctx:
        def sb(name, shape, dt=F32):
            return ctx.enter_context(nc.sbuf_tensor(name, shape, dt))

        def sem(name):
            return ctx.enter_context(nc.semaphore(name))

        wa_h, wa_l = sb("wa_h", [P, KC, 3 * C], F32R), sb("wa_l", [P, KC, 3 * C], F32R)
        wp_h, wp_l = sb("wp_h", [P, KC, C], F32R), sb("wp_l", [P, KC, C], F32R)
        win_h, win_l = sb("win_h", [P, KC, P], F32R), sb("win_l", [P, KC, P], F32R)
        wo_h, wo_l = sb("wo_h", [P, C], F32R), sb("wo_l", [P, C], F32R)
        hbout = sb("hbout", [P, C])
        ident, tri, bones = sb("ident", [P, P]), sb("tri", [P, P]), sb("bones", [P, P])
        ones = sb("ones", [1, P])
        w1c, b1c, w2c = sb("w1c", [P, HI]), sb("b1c", [P, HI]), sb("w2c", [P, HI])
        binc, b2c = sb("binc", [P, 1]), sb("b2c", [P, 1])
        mhalf = sb("mhalf", [P, TILES])

        res = [sb(f"res{i}", [P, TILES, C]) for i in range(SLOTS)]
        xhat = [sb(f"xhat{i}", [P, C]) for i in range(4)]
        xh, xl = sb("xh", [P, KC, BLK], F32R), sb("xl", [P, KC, BLK], F32R)
        qT, kT = sb("qT", [P, 4, BLK]), sb("kT", [P, 4, BLK])
        v = sb("v", [P, TILES, C])
        A = sb("A", [P, 4, 4, P])
        ktok = [sb(f"ktok{i}", [P, C]) for i in range(2)]
        S = sb("S", [P, 4, P])
        yh = [sb(f"yh{i}", [P, 4, P], F32R) for i in range(2)]
        yl = [sb(f"yl{i}", [P, 4, P], F32R) for i in range(2)]
        ffs = sb("ffs", [P, 2, BLK])
        ffr = [sb(f"ffr{i}", [P, 2, BLK]) for i in range(2)]
        acc = sb("acc", [P, 2, BLK])
        gh, gl = sb("gh", [P, 2, BLK], F32R), sb("gl", [P, 2, BLK], F32R)
        zc = sb("zc", [P, 4])
        st = sb("st", [P, 3, TILES, 6])
        mv = sb("mv", [P, 3, TILES, 2])
        rstd = sb("rstd", [P, 3, TILES])
        nmr = sb("nmr", [P, 3, TILES])
        e2, z2, rd2 = ffr[0], ffr[1], ffs

        bank = [ctx.enter_context(nc.psum_tensor(f"bank{i}", [P, 512], F32)) for i in range(8)]

        pe, act, dve, pool = (Queue(sem(n)) for n in ("s_pe", "s_act", "s_dve", "s_pool"))
        sp = Queue(sem("s_sp"))
        s_ld = [sem(f"s_ld{i}") for i in range(SLOTS)]
        s_st = [sem(f"s_st{i}") for i in range(SLOTS)]

        free = [None] * 8
        turn = [0]

        def take(ring):
            b = ring[turn[0] % len(ring)]
            turn[0] += 1
            pe.wait(free[b])
            return b

        LATE, EARLY = (5, 6, 7), (5, 6, 7, 0, 1, 2, 3)
        NUM = 4

        def f32(ap):
            return ap.bitcast(F32)

        def mm(o, l, r, start, stop, **kw):
            pe.put(lambda e: e.matmul(o, l, r, start=start, stop=stop, **kw))

        def mm_done(o, l, r, start, stop, **kw):
            return pe.do(lambda e: e.matmul(o, l, r, start=start, stop=stop, **kw))

        def split3(o, pairs):
            n = 3 * len(pairs)
            i = 0
            for lh, ll, rh, rl in pairs:
                for l, r in ((lh, rh), (lh, rl), (ll, rh)):
                    i += 1
                    f = mm if i < n else mm_done
                    done = f(o, l, r, i == 1, i == n)
            return done

        s_c = {}

        def load_const(name, dst, src):
            s_c[name] = sem(f"s_{name}")
            return sp.dma(lambda e: e.dma_start(dst, src), s_c[name], 16)

        loaded = {}

        def load(b):
            s = b % SLOTS
            if b >= SLOTS:
                sp.wait(stored[b - SLOTS])
            loaded[b] = sp.dma(lambda e: e.dma_start(res[s][:, :, :], xv[b]), s_ld[s], 16 * (b // SLOTS + 1))

        stored = {}

        def store(b, done):
            s = b % SLOTS
            sp.wait(done)
            stored[b] = sp.dma(lambda e: e.dma_start(ov[b], res[s][:, :, :]), s_st[s], 16 * (b // SLOTS + 1))

        win_v = Win.rearrange("(k p) m -> p k m", p=P)
        win_st = ffr[0][:, 0, :].rearrange("p (k m) -> p k m", k=KC)
        wo_st = ffr[1][:, 0, :]
        load(0)
        l_win0 = load_const("win0", win_st[:, :, 0:M], win_v)
        l_win1 = load_const("win1", win_st[:, :, M:P], win_v)
        l_wo0 = load_const("wo0", wo_st[0:M, :], Wout)
        l_wo1 = load_const("wo1", wo_st[M:P, :], Wout)
        l_small = []
        for name, dst, src in (("w1", w1c, W1), ("b1", b1c, b1), ("w2", w2c, W2)):
            for h in range(2):
                l_small.append(load_const(f"{name}{h}", dst[M * h:M * h + M, :], src[:, HI * h:HI * h + HI]))
        for h in range(2):
            l_small.append(load_const(f"bin{h}", binc[M * h:M * h + M, :], bin_.rearrange("(m a) -> m a", a=1)))
        z_b2 = pool.do(lambda e: e.memset(b2c[:, :], 0.0))
        sp.wait(z_b2)
        l_small.append(load_const("b2", b2c[0:M, :], b2.rearrange("(m a) -> m a", a=1)))
        l_bout = load_const("bout", acc[0:1, 0, :], bout.rearrange("(a n) -> a n", a=1))
        wa_v = w_attn.rearrange("(k p) n -> p k n", p=P)
        wa_st = [qT, kT, v]
        l_wa = {n: load_const(f"wa{n}", wa_st[n][:, :, :], wa_v[:, :, n * C:n * C + C]) for n in (1, 0, 2)}
        wp_st = A[:, :, :, :].rearrange("p h g n -> p h (g n)")
        l_wp = load_const("wp", wp_st, w_proj.rearrange("(k p) n -> p k n", p=P))
        load(1)
        load(2)

        z_id = pool.do(lambda e: e.memset(ident[:, :], 0.0))
        z_tri = pool.do(lambda e: e.memset(tri[:, :], 1.0))
        z_bones = pool.do(lambda e: e.memset(bones[:, :], 0.0))
        z_S = pool.do(lambda e: e.memset(S[:, :, :], 0.0))
        c_ones = pool.do(lambda e: e.memset(ones[:, :], 1.0))
        c_half = pool.do(lambda e: e.memset(mhalf[:, :], -0.5))
        pool.wait(z_id)
        c_ident = pool.do(lambda e: e.affine_select(out=ident[:, :], in_=ident[:, :], compare_op=ALU.not_equal, fill=1.0,
                                                    base=0, pattern=[[-1, P]], channel_multiplier=1))
        pool.wait(z_tri)
        c_tri = pool.do(lambda e: e.affine_select(out=tri[:, :], in_=tri[:, :], compare_op=ALU.is_ge, fill=0.0,
                                                  base=0, pattern=[[1, P]], channel_multiplier=-1))
        pool.wait(z_bones)
        pool.wait(c_tri)
        for h in range(4):
            if h:
                pool.wait(c_bones)
            c_bones = pool.do(lambda e, h=h: e.memset(bones[D * h:D * h + D, D * h:D * h + D], 1.0))

        pool.wait(c_bones)

        def split_weight(src, hi, lo, *ready):
            act.wait(*ready)
            h = act.do(lambda e: e.activation(hi, src, ACT.Copy))
            dve.wait(h, *ready)
            return dve.do(lambda e: e.tensor_tensor(lo, src, f32(hi), ALU.subtract))

        w_in = split_weight(win_st, win_h[:, :, :], win_l[:, :, :], l_win0, l_win1)
        w_out = split_weight(wo_st, wo_h[:, :], wo_l[:, :], l_wo0, l_wo1)
        w_a = {}

        pe.wait(l_bout, c_ones)
        b = take(EARLY)
        m_bout = mm_done(bank[b][:, :], ones[0:1, :], acc[0:1, 0, :], True, True)
        act.wait(m_bout)
        c_bout = act.do(lambda e, b=b: e.activation(hbout[:, :], bank[b][:, :], ACT.Copy, scale=0.5))
        free[b] = c_bout

        stats_done, norm_last = {}, [None] * 3
        resid = {}
        xhat_free = [None] * 4
        xturn = [0]
        xhat_ready = {}

        def ln_stats(n, b, t, ready):
            r = res[b % SLOTS]
            dve.wait(ready, norm_last[n])
            s = dve.do(lambda e: e.bn_stats(st[:, n, t, :], r[:, t, :]))
            dve.wait(s)
            aggr = dve.do(lambda e: e.bn_aggr(mv[:, n, t, :], st[:, n, t, :]))
            if t == TILES - 1:
                pool.wait(aggr, norm_last[n], c_half)
                ve = pool.do(lambda e: e.tensor_scalar(nmr[:, n, :], mv[:, n, :, 1], LN_EPS, None, ALU.add))
                pool.wait(ve)
                pw = pool.do(lambda e: e.tensor_tensor(rstd[:, n, :], nmr[:, n, :], mhalf[:, :], ALU.pow))
                dve.wait(pw, aggr)
                stats_done[n, b] = dve.do(lambda e: e.scalar_tensor_tensor(
                    nmr[:, n, :], mv[:, n, :, 0], -1.0, rstd[:, n, :], ALU.mult, ALU.mult))

        def normalise(n, b, t):
            i = xturn[0] % 4
            xturn[0] += 1
            r = res[b % SLOTS]
            act.wait(stats_done[n, b], xhat_free[i])
            done = act.do(lambda e: e.activation(xhat[i][:, :], r[:, t, :], ACT.Identity,
                                                 bias=nmr[:, n, t:t + 1], scale=rstd[:, n, t:t + 1]))
            xhat_ready[n, b, t] = (i, done)
            norm_last[n] = done

        xT_free = [None]
        xT_ready = {}

        def to_channels(n, b, t):
            i, ready = xhat_ready.pop((n, b, t))
            k = take(LATE)
            pe.wait(ready, c_ident)
            for c in range(KC):
                f = pe.do if c == KC - 1 else pe.put
                done = f(lambda e, c=c: e.transpose(bank[k][:, c * P:c * P + P], xhat[i][:, c * P:c * P + P], ident[:, :]))
            xhat_free[i] = done
            src = bank[k][:, :].rearrange("p (c t) -> p c t", c=KC)
            act.wait(done, xT_free[0])
            h = act.do(lambda e: e.activation(xh[:, :, t * P:t * P + P], src, ACT.Copy))
            dve.wait(h, xT_free[0])
            lo = dve.do(lambda e: e.tensor_tensor(xl[:, :, t * P:t * P + P], src, f32(xh[:, :, t * P:t * P + P]), ALU.subtract))
            free[k] = lo
            xT_ready[n, b] = (h, lo)

        def add_bias(b, after):
            r = res[b % SLOTS]
            bb = hbout[:, :].unsqueeze(1).to_broadcast([P, TILES, C])
            pool.wait(after, c_bout)
            return pool.do(lambda e: e.tensor_tensor(r[:, :, :], r[:, :, :], bb, ALU.add))

        ff = {"r_free": [None, None], "s_free": None, "acc_done": None, "g_free": None}

        def ff_in(n, b, half):
            k = take(LATE)
            pe.wait(w_in, *xT_ready[n, b])
            done = split3(bank[k][:, :], [(win_h[:, c, :], win_l[:, c, :], xh[:, c, :], xl[:, c, :]) for c in range(KC)])
            xT_free[0] = done
            act.wait(done, ff["s_free"], *l_small)
            s = act.do(lambda e: e.activation(ffs[:, half, :], bank[k][:, :], ACT.Identity, bias=binc[:, 0:1]))
            free[k] = s
            return s

        def ff_hidden(i, lo, hi, ready):
            r = ffr[i % 2]
            act.wait(ready, ff["r_free"][i % 2])
            a = act.do(lambda e: e.activation(r[:, lo:hi, :], ffs[:, lo:hi, :], ACT.Relu,
                                              bias=b1c[:, i:i + 1], scale=w1c[:, i:i + 1]))
            ff["s_free"] = a
            dve.wait(a, ff["acc_done"], *l_small)
            if i == 0:
                dve.wait(ff["g_done"] if "g_done" in ff else None, m_bout)
                d = dve.do(lambda e: e.tensor_scalar(acc[:, lo:hi, :], r[:, lo:hi, :], w2c[:, 0:1], b2c[:, 0:1],
                                                     ALU.mult, ALU.add))
            else:
                d = dve.do(lambda e: e.scalar_tensor_tensor(acc[:, lo:hi, :], r[:, lo:hi, :], w2c[:, i:i + 1],
                                                            acc[:, lo:hi, :], ALU.mult, ALU.add))
            ff["acc_done"] = ff["r_free"][i % 2] = d

        def ff_gate(lo, hi):
            act.wait(ff["acc_done"], ff["g_free"])
            h = act.do(lambda e: e.activation(gh[:, lo:hi, :], acc[:, lo:hi, :], ACT.Copy))
            dve.wait(h, ff["acc_done"], ff["g_free"])
            ff["g_done"] = dve.do(lambda e: e.tensor_tensor(gl[:, lo:hi, :], acc[:, lo:hi, :], f32(gh[:, lo:hi, :]), ALU.subtract))

        def ff_out(b, t, half, biased):
            k = take(LATE)
            pe.wait(ff["g_done"], w_out)
            w = slice(t * P, t * P + P)
            done = split3(bank[k][:, :], [(gh[:, half, w], gl[:, half, w], wo_h[:, :], wo_l[:, :])])
            ff["g_free"] = done
            r = res[b % SLOTS]
            dve.wait(done, biased)
            free[k] = dve.do(lambda e: e.scalar_tensor_tensor(r[:, t, :], bank[k][:, :], 0.5, r[:, t, :], ALU.mult, ALU.add))
            return free[k]

        at = {"kq_free": None, "v_free": [None] * TILES, "e_free": [None, None], "z_free": [None, None],
              "rd_free": [None, None], "zc": [None] * 4, "S": None, "S_free": None, "kt_free": [None, None],
              "A_free": None, "y_free": [None, None], "A": None}

        def project(g, which, b, u):
            dst = (qT, kT)[which]
            k = take(EARLY)
            col = which * C + g * P
            pe.wait(w_a[which], *xT_ready[2, b])
            done = split3(bank[k][:, :], [(wa_h[:, c, col:col + P], wa_l[:, c, col:col + P], xh[:, c, :], xl[:, c, :])
                                          for c in range(KC)])
            xT_free[0] = done
            ee = e2[:, u % 2, :]
            act.wait(done, at["e_free"][u % 2], ff["acc_done"], w_a[which], at["kq_free"])
            act.put(lambda e: e.activation(ee, bank[k][:, :], ACT.Exp))
            a = act.do(lambda e: e.activation(dst[:, g, :], bank[k][:, :], ACT.Identity, bias=1.0))
            free[k] = a
            dve.wait(a)
            f = dve.do(lambda e: e.scalar_tensor_tensor(dst[:, g, :], ee, 1.0, dst[:, g, :], ALU.min, ALU.max))
            at["e_free"][u % 2] = f
            return f

        def key_sums(g, b, k_ready, q_ready):
            z = z2[:, g % 2, :]
            first = b % PER == 0
            init = 0.0 if first else zc[:, g:g + 1]
            dve.wait(k_ready, at["z_free"][g % 2], ff["acc_done"], None if first else at["zc"][g])
            s = dve.do(lambda e: e.tensor_tensor_scan(z, kT[:, g, :], kT[:, g, :], init, ALU.add, ALU.bypass))
            pool.wait(s, q_ready)
            at["zc"][g] = pool.do(lambda e: e.tensor_copy(zc[:, g:g + 1], z[:, BLK - 1:BLK]))
            pool.wait(at["zc"][g])
            return pool.do(lambda e: e.tensor_tensor(z, qT[:, g, :], z, ALU.mult))

        def normalise_q(g, z_ready):
            z, rd = z2[:, g % 2, :], rd2[:, g % 2, :]
            k = take(EARLY)
            pe.wait(z_ready, c_bones)
            done = mm_done(bank[k][:, :], bones[:, :], z, True, True)
            at["z_free"][g % 2] = done
            act.wait(done, at["rd_free"][g % 2], ff["s_free"])
            a = act.do(lambda e: e.activation(rd, bank[k][:, :], ACT.Identity, bias=EPS))
            free[k] = a
            dve.wait(a)
            r = dve.do(lambda e: e.reciprocal(rd, rd))
            pool.wait(r)
            at["rd_free"][g % 2] = pool.do(lambda e: e.tensor_tensor(qT[:, g, :], qT[:, g, :], rd, ALU.mult))
            return at["rd_free"][g % 2]

        def values(b, t):
            k = take(EARLY)
            w = slice(t * P, t * P + P)
            pe.wait(w_a[2])
            done = split3(bank[k][:, :], [(xh[:, c, w], xl[:, c, w], wa_h[:, c, 2 * C:], wa_l[:, c, 2 * C:]) for c in range(KC)])
            xT_free[0] = done
            act.wait(done, at["v_free"][t], w_a[2])
            free[k] = act.do(lambda e: e.activation(v[:, t, :], bank[k][:, :], ACT.Copy))
            return free[k]

        def keys_by_token(t, k_ready):
            k = take(LATE)
            pe.wait(*k_ready, c_ident)
            w = slice(t * P, t * P + P)
            for g in range(4):
                f = pe.do if g == 3 else pe.put
                done = f(lambda e, g=g: e.transpose(bank[k][:, g * P:g * P + P], kT[:, g, w], ident[:, :]))
            at["kq_free"] = done
            act.wait(done, at["kt_free"][t % 2])
            free[k] = act.do(lambda e: e.activation(ktok[t % 2][:, :], bank[k][:, :], ACT.Copy))
            return free[k]

        def scores(t, qn_ready):
            w = slice(t * P, t * P + P)
            for h in range(4):
                pe.wait(free[h])
            pe.wait(*qn_ready)
            done = [None] * 4
            for g in range(4):
                for h in range(4):
                    d = slice(D * h, D * h + D)
                    f = mm_done if g == 3 else mm
                    done[h] = f(bank[h][:, g * P:g * P + P], kT[d, g, w], qT[d, g, w], True, True)
            at["kq_free"] = done[3]
            mask = tri[:, :].unsqueeze(1).to_broadcast([P, 4, P])
            dve.wait(c_tri, at["A_free"], w_p)
            for h in range(4):
                dve.wait(done[h])
                free[h] = dve.do(lambda e, h=h: e.tensor_tensor(
                    A[:, h, :, :], bank[h][:, :].rearrange("p (g i) -> p g i", g=4), mask, ALU.mult))
            at["A"] = free[3]

        def attend(t, b, v_ready):
            w = slice(t * P, t * P + P)
            first = b % PER == 0 and t == 0
            pe.wait(free[NUM])
            num = bank[NUM]
            if not first:
                pe.wait(at["S"])
                for g in range(4):
                    f = mm_done if g == 3 else mm
                    done = f(num[:, g * P:g * P + P], S[:, g, :], qT[:, g, w], g == 0, False, skip_group_check=True)
                at["S_free"] = at["kq_free"] = done
            pe.wait(at["A"], v_ready)
            for g in range(4):
                for h in range(4):
                    d = slice(D * h, D * h + D)
                    f = mm_done if (g, h) == (3, 3) else mm
                    done = f(num[d, g * P:g * P + P], v[:, t, (4 * g + h) * D:(4 * g + h + 1) * D], A[:, h, g, :],
                             first and g == 0, True, skip_group_check=True)
            at["A_free"] = at["v_free"][t] = done
            src = num[:, :].rearrange("p (g i) -> p g i", g=4)
            o = t % 2
            act.wait(done, at["y_free"][o])
            a = act.do(lambda e: e.activation(yh[o][:, :, :], src, ACT.Copy))
            dve.wait(a, at["y_free"][o])
            free[NUM] = dve.do(lambda e: e.tensor_tensor(yl[o][:, :, :], src, f32(yh[o][:, :, :]), ALU.subtract))
            return a, free[NUM]

        def update(t, b, kt_ready, v_ready):
            k = take(LATE)
            pe.wait(kt_ready, v_ready)
            for g in range(4):
                f = mm_done if g == 3 else mm
                done = f(bank[k][:, g * P:g * P + P], ktok[t % 2][:, g * P:g * P + P], v[:, t, g * P:g * P + P], True, True)
            at["kt_free"][t % 2] = at["v_free"][t] = done
            src = bank[k][:, :].rearrange("p (g n) -> p g n", g=4)
            first = b % PER == 0 and t == 0
            dve.wait(done, at["S_free"], at["S"], z_S)
            for h in range(4):
                d = slice(D * h, D * h + D)
                if first:
                    s = dve.do(lambda e, d=d: e.tensor_copy(S[d, :, d], src[d, :, d]))
                else:
                    s = dve.do(lambda e, d=d: e.tensor_tensor(S[d, :, d], src[d, :, d], S[d, :, d], ALU.add))
            at["S"] = free[k] = s

        def project_out(t, b, y_ready):
            k = take(LATE)
            o = t % 2
            pe.wait(*y_ready, w_p)
            done = split3(bank[k][:, :], [(yh[o][:, g, :], yl[o][:, g, :], wp_h[:, g, :], wp_l[:, g, :]) for g in range(4)])
            at["y_free"][o] = done
            r = res[b % SLOTS]
            dve.wait(done)
            free[k] = dve.do(lambda e: e.tensor_tensor(r[:, t, :], bank[k][:, :], r[:, t, :], ALU.add))
            return free[k]

        for t in range(TILES):
            ln_stats(0, 0, t, loaded[0])
        w_p = None
        for j in range(-1, NB + 1):
            mid = 0 <= j < NB
            last = 0 <= j - 1 < NB
            nxt = j + 1 < NB
            if j == 0:
                for n in (1, 0, 2):
                    w_a[n] = split_weight(wa_st[n][:, :, :], wa_h[:, :, n * C:n * C + C], wa_l[:, :, n * C:n * C + C], l_wa[n])
                w_p = split_weight(wp_st, wp_h[:, :, :], wp_l[:, :, :], l_wp)
            if mid:
                k_r, q_r, z_r, qn_r, v_r = {}, {}, {}, {}, {}
                for g in range(4):
                    k_r[g] = project(g, 1, j, 2 * g)
                    if g >= 1:
                        z_r[g - 1] = key_sums(g - 1, j, k_r[g - 1], q_r[g - 1])
                    q_r[g] = project(g, 0, j, 2 * g + 1)
                    if g >= 1:
                        qn_r[g - 1] = normalise_q(g - 1, z_r[g - 1])
                    if nxt:
                        ln_stats(0, j + 1, g, loaded[j + 1])
                    if last:
                        normalise(1, j - 1, g)
                z_r[3] = key_sums(3, j, k_r[3], q_r[3])
                v_r[0] = values(j, 0)
                v_r[1] = values(j, 1)
                qn_r[3] = normalise_q(3, z_r[3])
                v_r[2] = values(j, 2)
                v_r[3] = values(j, 3)
            elif last:
                for t in range(TILES):
                    normalise(1, j - 1, t)

            ffs_ready = []
            lo, hi = (0 if last else 1), (2 if nxt else 1)
            biased = {}

            def hidden(*idx):
                if last or nxt:
                    for i in idx:
                        act.wait(*ffs_ready)
                        ff_hidden(i, lo, hi, ffs_ready[-1])

            if last:
                for t in range(TILES):
                    to_channels(1, j - 1, t)
                biased[j - 1] = add_bias(j - 1, norm_last[1])
            if nxt:
                for t in range(TILES):
                    normalise(0, j + 1, t)
                biased[j + 1] = add_bias(j + 1, norm_last[0])
            if mid:
                kt = {0: keys_by_token(0, list(k_r.values()))}
                scores(0, list(qn_r.values()))
            if last:
                ffs_ready.append(ff_in(1, j - 1, 0))
            if nxt:
                for t in range(TILES):
                    to_channels(0, j + 1, t)
            y = {}
            lnq = []

            def inner(t):
                y[t] = attend(t, j, v_r[t])
                if not ((j + 1) % PER == 0 and t == TILES - 1):
                    update(t, j, kt[t], v_r[t])

            def outer(t):
                r = project_out(t, j, y[t])
                ln_stats(1, j, t, r)

            if mid:
                inner(0)
            if nxt:
                ffs_ready.append(ff_in(0, j + 1, 1))
            if mid:
                kt[1] = keys_by_token(1, [])
                scores(1, [])
            hidden(0, 1)
            if mid:
                outer(0)
            hidden(2)
            if mid:
                inner(1)
            hidden(3)
            if mid:
                kt[2] = keys_by_token(2, [])
                scores(2, [])
            hidden(4)
            if mid:
                outer(1)
            hidden(5)
            if mid:
                inner(2)
            hidden(6)
            if mid:
                kt[3] = keys_by_token(3, [])
                scores(3, [])
            hidden(7)
            if last or nxt:
                ff_gate(lo, hi)
            if mid:
                outer(2)
            if nxt:
                for t in range(TILES):
                    r = ff_out(j + 1, t, 1, biased[j + 1])
                    ln_stats(2, j + 1, t, r)
            if mid:
                inner(3)
            if nxt:
                for t in range(TILES):
                    normalise(2, j + 1, t)
            if last:
                for t in range(TILES):
                    r = ff_out(j - 1, t, 0, biased[j - 1])
                store(j - 1, r)
            if nxt:
                for t in range(TILES):
                    to_channels(2, j + 1, t)
            if mid:
                outer(3)
            if 3 <= j + 3 < NB:
                load(j + 3)
        for b in range(NB - SLOTS, NB):
            sp.wait(stored[b])

        block = ctx.enter_context(nc.Block())

        @block.sync
        def _(eng):
            sp.run(eng)

        @block.gpsimd
        def _(eng):
            pool.run(eng)

        @block.scalar
        def _(eng):
            act.run(eng)

        @block.vector
        def _(eng):
            dve.run(eng)

        @block.tensor
        def _(eng):
            pe.run(eng)


_INS = ["L0_attn_x", "L0_attn_w_attn", "L0_attn_w_proj", "L0_ffn_Win", "L0_ffn_bin_", "L0_ffn_W1", "L0_ffn_b1",
        "L0_ffn_W2", "L0_ffn_b2", "L0_ffn_Wout", "L0_ffn_bout"]
_OUTS = [((16, 1024, 512), "float32")]


def kernel(**inputs):
    import numpy as _np
    import concourse.bacc as _bacc
    from concourse import mybir as _mybir
    from concourse.bass_utils import run_bass_kernel_spmd as _run

    nc = _bacc.Bacc("TRN2", target_bir_lowering=False, num_devices=1)
    arrays, args = {}, []
    for name in _INS:
        a = _np.ascontiguousarray(inputs[name])
        arrays[f"in_{name}_dram"] = a
        args.append(nc.dram_tensor(f"in_{name}_dram", a.shape, _mybir.dt.from_np(a.dtype), kind="ExternalInput").ap())
    for i, (shape, dtype) in enumerate(_OUTS):
        dt = _mybir.dt.from_np(_np.dtype(dtype))
        args.append(nc.dram_tensor(f"out_{i}_dram", shape, dt, kind="ExternalOutput").ap())
    macaron_kernel(nc, *args)
    r = _run(nc, [arrays], core_ids=[0])
    return r.results[0]["out_0_dram"]
```

```python
from contextlib import ExitStack

import concourse.bass as bass
from concourse import mybir

F32 = mybir.dt.float32
F32R = mybir.dt.float32r
ALU = mybir.AluOpType
ACT = mybir.ActivationFunctionType

P = 128
TILES = 4
BLK = P * TILES
SLOTS = 4


class Queue:

    def __init__(self, sem):
        self.sem, self.count, self.ops, self.seen = sem, 0, [], {}

    def wait(self, *marks):
        for mark in marks:
            if mark is None:
                continue
            sem, value = mark
            if self.seen.get(id(sem), 0) < value:
                self.seen[id(sem)] = value
                self.ops.append(lambda e, sem=sem, value=value: e.wait_ge(sem, value))

    def put(self, fn):
        self.ops.append(fn)

    def do(self, fn):
        self.count += 1
        sem = self.sem
        self.ops.append(lambda e: fn(e).then_inc(sem, 1))
        return sem, self.count

    def dma(self, fn, sem, total):
        self.ops.append(lambda e: fn(e).then_inc(sem, 16))
        return sem, total

    def run(self, eng):
        for op in self.ops:
            op(eng)


def macaron_kernel(nc, x, w_attn, w_proj, Win, bin_, W1, b1, W2, b2, Wout, bout, out):
    B, T, C = x.shape
    M, INNER = W1.shape
    D = 32
    KC = C // P
    NB = B * T // BLK
    PER = T // BLK
    HI = INNER // 2
    LN_EPS, EPS = 1e-5, 1e-6
    assert C == 512 and M == 64 and INNER == 16 and T % BLK == 0

    xv = x.rearrange("b t c -> (b t) c").rearrange("(k q p) c -> k p q c", q=TILES, p=P)
    ov = out.rearrange("b t c -> (b t) c").rearrange("(k q p) c -> k p q c", q=TILES, p=P)

    ctx = ExitStack()
    with ctx:
        def sb(name, shape, dt=F32):
            return ctx.enter_context(nc.sbuf_tensor(name, shape, dt))

        def sem(name):
            return ctx.enter_context(nc.semaphore(name))

        wa_h, wa_l = sb("wa_h", [P, KC, 3 * C], F32R), sb("wa_l", [P, KC, 3 * C], F32R)
        wp_h, wp_l = sb("wp_h", [P, KC, C], F32R), sb("wp_l", [P, KC, C], F32R)
        win_h, win_l = sb("win_h", [P, KC, P], F32R), sb("win_l", [P, KC, P], F32R)
        wo_h, wo_l = sb("wo_h", [P, C], F32R), sb("wo_l", [P, C], F32R)
        hbout = sb("hbout", [P, C])
        ident, tri, bones = sb("ident", [P, P]), sb("tri", [P, P]), sb("bones", [P, P])
        ones = sb("ones", [1, P])
        w1c, b1c, w2c = sb("w1c", [P, HI]), sb("b1c", [P, HI]), sb("w2c", [P, HI])
        binc, b2c = sb("binc", [P, 1]), sb("b2c", [P, 1])
        mhalf = sb("mhalf", [P, TILES])

        res = [sb(f"res{i}", [P, TILES, C]) for i in range(SLOTS)]
        xhat = [sb(f"xhat{i}", [P, C]) for i in range(4)]
        xh, xl = sb("xh", [P, KC, BLK], F32R), sb("xl", [P, KC, BLK], F32R)
        qT, kT = sb("qT", [P, 4, BLK]), sb("kT", [P, 4, BLK])
        v = sb("v", [P, TILES, C])
        A = sb("A", [P, 4, 4, P])
        ktok = [sb(f"ktok{i}", [P, C]) for i in range(2)]
        S = sb("S", [P, 4, P])
        yh = [sb(f"yh{i}", [P, 4, P], F32R) for i in range(2)]
        yl = [sb(f"yl{i}", [P, 4, P], F32R) for i in range(2)]
        ffs = sb("ffs", [P, 2, BLK])
        ffr = [sb(f"ffr{i}", [P, 2, BLK]) for i in range(2)]
        acc = sb("acc", [P, 2, BLK])
        gh, gl = sb("gh", [P, 2, BLK], F32R), sb("gl", [P, 2, BLK], F32R)
        zc = sb("zc", [P, 4])
        st = sb("st", [P, 3, TILES, 6])
        mv = sb("mv", [P, 3, TILES, 2])
        rstd = sb("rstd", [P, 3, TILES])
        nmr = sb("nmr", [P, 3, TILES])
        rd2 = sb("rd2", [P, 2, BLK])
        e2, z2 = ffr[0], ffr[1]

        bank = [ctx.enter_context(nc.psum_tensor(f"bank{i}", [P, 512], F32)) for i in range(8)]

        pe, act, dve, pool = (Queue(sem(n)) for n in ("s_pe", "s_act", "s_dve", "s_pool"))
        sp = Queue(sem("s_sp"))
        s_ld = [sem(f"s_ld{i}") for i in range(SLOTS)]
        s_st = [sem(f"s_st{i}") for i in range(SLOTS)]

        free = [None] * 8
        turn = [0]
        busy = set()

        def take(ring):
            free_of = [b for b in ring if b not in busy]
            b = free_of[turn[0] % len(free_of)]
            turn[0] += 1
            pe.wait(free[b])
            return b

        LATE, EARLY = (5, 6, 7), (5, 6, 7, 0, 1, 2, 3)
        NUM = 4

        def f32(ap):
            return ap.bitcast(F32)

        def mm(o, l, r, start, stop, **kw):
            pe.put(lambda e: e.matmul(o, l, r, start=start, stop=stop, **kw))

        def mm_done(o, l, r, start, stop, **kw):
            return pe.do(lambda e: e.matmul(o, l, r, start=start, stop=stop, **kw))

        def split3(o, pairs, first=True, last=True):
            n = 3 * len(pairs)
            i = 0
            for lh, ll, rh, rl in pairs:
                for l, r in ((lh, rh), (lh, rl), (ll, rh)):
                    i += 1
                    f = mm if i < n else mm_done
                    done = f(o, l, r, first and i == 1, last and i == n)
            return done

        s_c = {}

        def load_const(name, dst, src):
            s_c[name] = sem(f"s_{name}")
            return sp.dma(lambda e: e.dma_start(dst, src), s_c[name], 16)

        loaded = {}

        def load(b):
            s = b % SLOTS
            if b >= SLOTS:
                sp.wait(stored[b - SLOTS])
            loaded[b] = sp.dma(lambda e: e.dma_start(res[s][:, :, :], xv[b]), s_ld[s], 16 * (b // SLOTS + 1))

        stored = {}

        def store(b, done):
            s = b % SLOTS
            sp.wait(done)
            stored[b] = sp.dma(lambda e: e.dma_start(ov[b], res[s][:, :, :]), s_st[s], 16 * (b // SLOTS + 1))

        win_v = Win.rearrange("(k p) m -> p k m", p=P)
        win_st = ffr[0][:, 0, :].rearrange("p (k m) -> p k m", k=KC)
        wo_st = ffr[1][:, 0, :]
        load(0)
        l_win0 = load_const("win0", win_st[:, :, 0:M], win_v)
        l_win1 = load_const("win1", win_st[:, :, M:P], win_v)
        l_wo0 = load_const("wo0", wo_st[0:M, :], Wout)
        l_wo1 = load_const("wo1", wo_st[M:P, :], Wout)
        l_small = []
        for name, dst, src in (("w1", w1c, W1), ("b1", b1c, b1), ("w2", w2c, W2)):
            for h in range(2):
                l_small.append(load_const(f"{name}{h}", dst[M * h:M * h + M, :], src[:, HI * h:HI * h + HI]))
        for h in range(2):
            l_small.append(load_const(f"bin{h}", binc[M * h:M * h + M, :], bin_.rearrange("(m a) -> m a", a=1)))
        z_b2 = pool.do(lambda e: e.memset(b2c[:, :], 0.0))
        sp.wait(z_b2)
        l_small.append(load_const("b2", b2c[0:M, :], b2.rearrange("(m a) -> m a", a=1)))
        l_bout = load_const("bout", acc[0:1, 0, :], bout.rearrange("(a n) -> a n", a=1))
        wa_v = w_attn.rearrange("(k p) n -> p k n", p=P)
        wa_st = [qT, kT, v]
        l_wa = {n: load_const(f"wa{n}", wa_st[n][:, :, :], wa_v[:, :, n * C:n * C + C]) for n in (1, 0, 2)}
        wp_st = A[:, :, :, :].rearrange("p h g n -> p h (g n)")
        l_wp = load_const("wp", wp_st, w_proj.rearrange("(k p) n -> p k n", p=P))
        load(1)
        load(2)

        z_id = pool.do(lambda e: e.memset(ident[:, :], 0.0))
        z_tri = pool.do(lambda e: e.memset(tri[:, :], 1.0))
        z_bones = pool.do(lambda e: e.memset(bones[:, :], 0.0))
        z_S = pool.do(lambda e: e.memset(S[:, :, :], 0.0))
        c_ones = pool.do(lambda e: e.memset(ones[:, :], 1.0))
        c_half = pool.do(lambda e: e.memset(mhalf[:, :], -0.5))
        pool.wait(z_id)
        c_ident = pool.do(lambda e: e.affine_select(out=ident[:, :], in_=ident[:, :], compare_op=ALU.not_equal, fill=1.0,
                                                    base=0, pattern=[[-1, P]], channel_multiplier=1))
        pool.wait(z_tri)
        c_tri = pool.do(lambda e: e.affine_select(out=tri[:, :], in_=tri[:, :], compare_op=ALU.is_ge, fill=0.0,
                                                  base=0, pattern=[[1, P]], channel_multiplier=-1))
        pool.wait(z_bones)
        pool.wait(c_tri)
        for h in range(4):
            if h:
                pool.wait(c_bones)
            c_bones = pool.do(lambda e, h=h: e.memset(bones[D * h:D * h + D, D * h:D * h + D], 1.0))

        pool.wait(c_bones)

        def split_weight(src, hi, lo, *ready):
            act.wait(*ready)
            h = act.do(lambda e: e.activation(hi, src, ACT.Copy))
            dve.wait(h, *ready)
            return dve.do(lambda e: e.tensor_tensor(lo, src, f32(hi), ALU.subtract))

        w_in = split_weight(win_st, win_h[:, :, :], win_l[:, :, :], l_win0, l_win1)
        w_out = split_weight(wo_st, wo_h[:, :], wo_l[:, :], l_wo0, l_wo1)
        w_a = {}

        pe.wait(l_bout, c_ones)
        b = take(EARLY)
        m_bout = mm_done(bank[b][:, :], ones[0:1, :], acc[0:1, 0, :], True, True)
        act.wait(m_bout)
        c_bout = act.do(lambda e, b=b: e.activation(hbout[:, :], bank[b][:, :], ACT.Copy, scale=0.5))
        free[b] = c_bout

        stats_done, norm_last = {}, [None] * 3
        resid = {}
        xhat_free = [None] * 4
        xturn = [0]
        xhat_ready = {}

        def ln_stats(n, b, t, ready):
            r = res[b % SLOTS]
            dve.wait(ready, norm_last[n])
            s = dve.do(lambda e: e.bn_stats(st[:, n, t, :], r[:, t, :]))
            dve.wait(s)
            aggr = dve.do(lambda e: e.bn_aggr(mv[:, n, t, :], st[:, n, t, :]))
            if t == TILES - 1:
                pool.wait(aggr, norm_last[n], c_half)
                ve = pool.do(lambda e: e.tensor_scalar(nmr[:, n, :], mv[:, n, :, 1], LN_EPS, None, ALU.add))
                pool.wait(ve)
                pw = pool.do(lambda e: e.tensor_tensor(rstd[:, n, :], nmr[:, n, :], mhalf[:, :], ALU.pow))
                dve.wait(pw, aggr)
                stats_done[n, b] = dve.do(lambda e: e.scalar_tensor_tensor(
                    nmr[:, n, :], mv[:, n, :, 0], -1.0, rstd[:, n, :], ALU.mult, ALU.mult))

        def normalise(n, b, t):
            i = xturn[0] % 4
            xturn[0] += 1
            r = res[b % SLOTS]
            act.wait(stats_done[n, b], xhat_free[i])
            done = act.do(lambda e: e.activation(xhat[i][:, :], r[:, t, :], ACT.Identity,
                                                 bias=nmr[:, n, t:t + 1], scale=rstd[:, n, t:t + 1]))
            xhat_ready[n, b, t] = (i, done)
            norm_last[n] = done

        xT_free = [None]
        xT_ready = {}

        def to_channels(n, b, t):
            i, ready = xhat_ready.pop((n, b, t))
            k = take(LATE)
            pe.wait(ready, c_ident)
            for c in range(KC):
                f = pe.do if c == KC - 1 else pe.put
                done = f(lambda e, c=c: e.transpose(bank[k][:, c * P:c * P + P], xhat[i][:, c * P:c * P + P], ident[:, :]))
            xhat_free[i] = done
            src = bank[k][:, :].rearrange("p (c t) -> p c t", c=KC)
            act.wait(done, xT_free[0])
            h = act.do(lambda e: e.activation(xh[:, :, t * P:t * P + P], src, ACT.Copy))
            dve.wait(h, xT_free[0])
            lo = dve.do(lambda e: e.tensor_tensor(xl[:, :, t * P:t * P + P], src, f32(xh[:, :, t * P:t * P + P]), ALU.subtract))
            free[k] = lo
            xT_ready[n, b] = (h, lo)

        def add_bias(b, t, after):
            r = res[b % SLOTS]
            pool.wait(after, c_bout)
            return pool.do(lambda e: e.tensor_tensor(r[:, t, :], r[:, t, :], hbout[:, :], ALU.add))

        ff = {"r_free": [None, None], "s_free": None, "acc_done": None, "g_free": None}

        def chunk_to_channels(n, b, c, ring):
            k, o = take(ring), c % 2
            pe.wait(c_ident)
            for t in range(TILES):
                i, ready = xhat_ready[n, b, t]
                pe.wait(ready)
                f = pe.do if t == TILES - 1 else pe.put
                done = f(lambda e, t=t, i=i: e.transpose(bank[k][:, t * P:t * P + P], xhat[i][:, c * P:c * P + P], ident[:, :]))
            if c == KC - 1:
                for t in range(TILES):
                    xhat_free[xhat_ready.pop((n, b, t))[0]] = done
            src = bank[k][:, :].rearrange("p (g t) -> p g t", g=4)
            act.wait(done, at["y_free"][o])
            h = act.do(lambda e: e.activation(yh[o][:, :, :], src, ACT.Copy))
            dve.wait(h, at["y_free"][o])
            free[k] = dve.do(lambda e: e.tensor_tensor(yl[o][:, :, :], src, f32(yh[o][:, :, :]), ALU.subtract))
            ff["chunk", c] = (h, free[k])

        def ff_in(half, c):
            k, o = NUM, c % 2
            if c == 0:
                pe.wait(free[k])
            pe.wait(w_in, *ff["chunk", c])
            flat = [x[:, :, :].rearrange("p g t -> p (g t)") for x in (yh[o], yl[o])]
            done = split3(bank[k][:, :], [(win_h[:, c, :], win_l[:, c, :], *flat)], c == 0, c == KC - 1)
            at["y_free"][o] = done
            if c == KC - 1:
                act.wait(done, ff["s_free"], *l_small)
                free[k] = act.do(lambda e: e.activation(ffs[:, half, :], bank[k][:, :], ACT.Identity, bias=binc[:, 0:1]))
                return free[k]

        def ff_hidden(i, lo, hi, ready):
            r = ffr[i % 2]
            act.wait(ready, ff["r_free"][i % 2], *at[("e_free", "z_free")[i % 2]])
            a = act.do(lambda e: e.activation(r[:, lo:hi, :], ffs[:, lo:hi, :], ACT.Relu,
                                              bias=b1c[:, i:i + 1], scale=w1c[:, i:i + 1]))
            ff["s_free"] = a
            dve.wait(a, ff["acc_done"], *l_small)
            if i == 0:
                dve.wait(ff["g_done"] if "g_done" in ff else None, m_bout)
                d = dve.do(lambda e: e.tensor_scalar(acc[:, lo:hi, :], r[:, lo:hi, :], w2c[:, 0:1], b2c[:, 0:1],
                                                     ALU.mult, ALU.add))
            else:
                d = dve.do(lambda e: e.scalar_tensor_tensor(acc[:, lo:hi, :], r[:, lo:hi, :], w2c[:, i:i + 1],
                                                            acc[:, lo:hi, :], ALU.mult, ALU.add))
            ff["acc_done"] = ff["r_free"][i % 2] = d

        def ff_gate(lo, hi):
            act.wait(ff["acc_done"], ff["g_free"])
            h = act.do(lambda e: e.activation(gh[:, lo:hi, :], acc[:, lo:hi, :], ACT.Copy))
            dve.wait(h, ff["acc_done"], ff["g_free"])
            ff["g_done"] = dve.do(lambda e: e.tensor_tensor(gl[:, lo:hi, :], acc[:, lo:hi, :], f32(gh[:, lo:hi, :]), ALU.subtract))

        def ff_out(b, t, half, biased, ring=LATE):
            k = take(ring)
            pe.wait(ff["g_done"], w_out)
            w = slice(t * P, t * P + P)
            done = split3(bank[k][:, :], [(gh[:, half, w], gl[:, half, w], wo_h[:, :], wo_l[:, :])])
            ff["g_free"] = done
            r = res[b % SLOTS]
            dve.wait(done, biased)
            free[k] = dve.do(lambda e: e.scalar_tensor_tensor(r[:, t, :], bank[k][:, :], 0.5, r[:, t, :], ALU.mult, ALU.add))
            return free[k]

        at = {"kq_free": None, "v_free": [None] * TILES, "e_free": [None, None], "z_free": [None, None],
              "rd_free": [None, None], "zc": [None] * 4, "S": None, "S_free": None, "kt_free": [None, None],
              "A_free": None, "y_free": [None, None], "A": None}

        def project(g, which, b, u):
            dst = (qT, kT)[which]
            k = take(EARLY)
            col = which * C + g * P
            pe.wait(w_a[which], *xT_ready[2, b])
            done = split3(bank[k][:, :], [(wa_h[:, c, col:col + P], wa_l[:, c, col:col + P], xh[:, c, :], xl[:, c, :])
                                          for c in range(KC)])
            xT_free[0] = done
            ee = e2[:, u % 2, :]
            act.wait(done, at["e_free"][u % 2], ff["acc_done"], w_a[which], at["kq_free"])
            act.put(lambda e: e.activation(ee, bank[k][:, :], ACT.Exp))
            a = act.do(lambda e: e.activation(dst[:, g, :], bank[k][:, :], ACT.Identity, bias=1.0))
            free[k] = a
            dve.wait(a)
            f = dve.do(lambda e: e.scalar_tensor_tensor(dst[:, g, :], ee, 1.0, dst[:, g, :], ALU.min, ALU.max))
            at["e_free"][u % 2] = f
            return f

        def key_sums(g, b, k_ready, q_ready):
            z = z2[:, g % 2, :]
            first = b % PER == 0
            init = 0.0 if first else zc[:, g:g + 1]
            dve.wait(k_ready, at["z_free"][g % 2], ff["acc_done"], None if first else at["zc"][g])
            s = dve.do(lambda e: e.tensor_tensor_scan(z, kT[:, g, :], kT[:, g, :], init, ALU.add, ALU.bypass))
            pool.wait(s, q_ready)
            at["zc"][g] = pool.do(lambda e: e.tensor_copy(zc[:, g:g + 1], z[:, BLK - 1:BLK]))
            pool.wait(at["zc"][g])
            return pool.do(lambda e: e.tensor_tensor(z, qT[:, g, :], z, ALU.mult))

        def denominator(g, z_ready):
            z, rd = z2[:, g % 2, :], rd2[:, g % 2, :]
            k = take(EARLY)
            pe.wait(z_ready, c_bones)
            done = mm_done(bank[k][:, :], bones[:, :], z, True, True)
            at["z_free"][g % 2] = done
            act.wait(done, at["rd_free"][g % 2])
            a = act.do(lambda e: e.activation(rd, bank[k][:, :], ACT.Identity, bias=EPS))
            free[k] = a
            return a

        def normalise_q(g, half, ready):
            w = slice(half * (BLK // 2), (half + 1) * (BLK // 2))
            rd = rd2[:, g % 2, w]
            dve.wait(ready)
            r = dve.do(lambda e: e.reciprocal(rd, rd))
            pool.wait(r)
            at["rd_free"][g % 2] = pool.do(lambda e: e.tensor_tensor(qT[:, g, w], qT[:, g, w], rd, ALU.mult))
            return at["rd_free"][g % 2]

        def values(b, t, part, ring, k=None):
            if part == 0:
                k = take(ring)
            w = slice(t * P, t * P + P)
            pe.wait(w_a[2])
            done = split3(bank[k][:, :], [(xh[:, c, w], xl[:, c, w], wa_h[:, c, 2 * C:], wa_l[:, c, 2 * C:])
                                          for c in (2 * part, 2 * part + 1)], part == 0, part == 1)
            if part == 0:
                busy.add(k)
                return k
            busy.remove(k)
            xT_free[0] = done
            act.wait(done, at["v_free"][t], w_a[2])
            free[k] = act.do(lambda e: e.activation(v[:, t, :], bank[k][:, :], ACT.Copy))
            return free[k]

        def keys_by_token(t, k_ready):
            k = take(LATE)
            pe.wait(*k_ready, c_ident)
            w = slice(t * P, t * P + P)
            for g in range(4):
                f = pe.do if g == 3 else pe.put
                done = f(lambda e, g=g: e.transpose(bank[k][:, g * P:g * P + P], kT[:, g, w], ident[:, :]))
            at["kq_free"] = done
            act.wait(done, at["kt_free"][t % 2])
            free[k] = act.do(lambda e: e.activation(ktok[t % 2][:, :], bank[k][:, :], ACT.Copy))
            return free[k]

        def scores(t, part, qn_ready):
            w = slice(t * P, t * P + P)
            heads = (0, 1) if part < 2 else (2, 3)
            if part % 2 == 0:
                busy.update(heads)
                for h in heads:
                    pe.wait(free[h])
            pe.wait(*qn_ready)
            done = {}
            for g in ((0, 1), (2, 3))[part % 2]:
                for h in heads:
                    d = slice(D * h, D * h + D)
                    f = mm_done if g == 3 else mm
                    done[h] = f(bank[h][:, g * P:g * P + P], kT[d, g, w], qT[d, g, w], True, True)
            if part % 2 == 0:
                return
            busy.difference_update(heads)
            at["kq_free"] = done[heads[1]]
            mask = tri[:, :].unsqueeze(1).to_broadcast([P, 4, P])
            dve.wait(c_tri, at["A_free"], w_p)
            for h in heads:
                dve.wait(done[h])
                free[h] = dve.do(lambda e, h=h: e.tensor_tensor(
                    A[:, h, :, :], bank[h][:, :].rearrange("p (g i) -> p g i", g=4), mask, ALU.mult))
            at["A"] = free[heads[1]]

        def attend(t, b, v_ready):
            w = slice(t * P, t * P + P)
            first = b % PER == 0 and t == 0
            pe.wait(free[NUM])
            num = bank[NUM]
            if not first:
                pe.wait(at["S"])
                for g in range(4):
                    f = mm_done if g == 3 else mm
                    done = f(num[:, g * P:g * P + P], S[:, g, :], qT[:, g, w], g == 0, False, skip_group_check=True)
                at["S_free"] = at["kq_free"] = done
            pe.wait(at["A"], v_ready)
            for g in range(4):
                for h in range(4):
                    d = slice(D * h, D * h + D)
                    f = mm_done if (g, h) == (3, 3) else mm
                    done = f(num[d, g * P:g * P + P], v[:, t, (4 * g + h) * D:(4 * g + h + 1) * D], A[:, h, g, :],
                             first and g == 0, True, skip_group_check=True)
            at["A_free"] = at["v_free"][t] = done
            src = num[:, :].rearrange("p (g i) -> p g i", g=4)
            o = t % 2
            act.wait(done, at["y_free"][o])
            a = act.do(lambda e: e.activation(yh[o][:, :, :], src, ACT.Copy))
            dve.wait(a, at["y_free"][o])
            free[NUM] = dve.do(lambda e: e.tensor_tensor(yl[o][:, :, :], src, f32(yh[o][:, :, :]), ALU.subtract))
            return a, free[NUM]

        def update(t, b, kt_ready, v_ready):
            k = take(LATE)
            pe.wait(kt_ready, v_ready)
            for g in range(4):
                f = mm_done if g == 3 else mm
                done = f(bank[k][:, g * P:g * P + P], ktok[t % 2][:, g * P:g * P + P], v[:, t, g * P:g * P + P], True, True)
            at["kt_free"][t % 2] = at["v_free"][t] = done
            src = bank[k][:, :].rearrange("p (g n) -> p g n", g=4)
            first = b % PER == 0 and t == 0
            dve.wait(done, at["S_free"], at["S"], z_S)
            for h in range(4):
                d = slice(D * h, D * h + D)
                if first:
                    s = dve.do(lambda e, d=d: e.tensor_copy(S[d, :, d], src[d, :, d]))
                else:
                    s = dve.do(lambda e, d=d: e.tensor_tensor(S[d, :, d], src[d, :, d], S[d, :, d], ALU.add))
            at["S"] = free[k] = s

        def project_out(t, b, y_ready, part, k=None):
            if part == 0:
                k = take(LATE)
            o = t % 2
            pe.wait(*y_ready, w_p)
            done = split3(bank[k][:, :], [(yh[o][:, g, :], yl[o][:, g, :], wp_h[:, g, :], wp_l[:, g, :])
                                          for g in (2 * part, 2 * part + 1)], part == 0, part == 1)
            if part == 0:
                busy.add(k)
                return k
            busy.remove(k)
            at["y_free"][o] = done
            r = res[b % SLOTS]
            dve.wait(done)
            free[k] = dve.do(lambda e: e.tensor_tensor(r[:, t, :], bank[k][:, :], r[:, t, :], ALU.add))
            return free[k]

        for t in range(TILES):
            ln_stats(0, 0, t, loaded[0])
        w_p = None
        biased, normed = {}, {}
        load(3)
        for j in range(-1, NB + 2):
            mid = 0 <= j < NB
            last = 0 <= j - 1 < NB
            nxt = j + 1 < NB
            if j == 0:
                for n in (1, 0, 2):
                    w_a[n] = split_weight(wa_st[n][:, :, :], wa_h[:, :, n * C:n * C + C], wa_l[:, :, n * C:n * C + C], l_wa[n])
                w_p = split_weight(wp_st, wp_h[:, :, :], wp_l[:, :, :], l_wp)
            k_r, q_r, z_r, d_r, qn_r, v_r, kt, y, held, ffs_ready = {}, {}, {}, {}, {}, {}, {}, {}, {}, []
            lo, hi = (0 if last else 1), (2 if nxt else 1)

            def chunk(half, c, ring=EARLY):
                if half == 0 and last:
                    chunk_to_channels(1, j - 1, c, ring)
                if half == 1 and nxt:
                    chunk_to_channels(0, j + 1, c, ring)

            def fin(half, c):
                if (nxt if half else last):
                    done = ff_in(half, c)
                    if c == KC - 1:
                        ffs_ready.append(done)

            def norm3():
                if last:
                    for t in range(TILES):
                        normalise(1, j - 1, t)
                    normed[j - 1] = norm_last[1]

            def norm1():
                if nxt:
                    for t in range(TILES):
                        normalise(0, j + 1, t)
                    normed[j + 1] = norm_last[0]

            def bias(half, t):
                if (nxt if half else last):
                    b = j + 1 if half else j - 1
                    biased[b] = add_bias(b, t, normed[b])

            def norm2():
                if nxt:
                    for t in range(TILES):
                        normalise(2, j + 1, t)

            def f1(*tiles):
                if nxt:
                    for t in tiles:
                        r = ff_out(j + 1, t, 1, biased[j + 1])
                        ln_stats(2, j + 1, t, r)

            def f2(b, *tiles):
                if 0 <= b < NB:
                    for t in tiles:
                        r = ff_out(b, t, 0, biased[b])
                        if t == TILES - 1:
                            store(b, r)
                            if b + 4 < NB:
                                load(b + 4)

            def t2(*tiles):
                if nxt:
                    for t in tiles:
                        to_channels(2, j + 1, t)

            def hidden(*idx):
                if last or nxt:
                    for i in idx:
                        act.wait(*ffs_ready)
                        ff_hidden(i, lo, hi, ffs_ready[-1])
                        if i == HI - 1:
                            ff_gate(lo, hi)

            def keys(g):
                if mid:
                    k_r[g] = project(g, 1, j, 2 * g)

            def queries(g):
                if mid:
                    q_r[g] = project(g, 0, j, 2 * g + 1)
                    z_r[g] = key_sums(g, j, k_r[g], q_r[g])

            def den(g):
                if mid:
                    d_r[g] = denominator(g, z_r[g])

            def rec(g, half):
                if mid:
                    qn_r[g] = normalise_q(g, half, d_r[g])

            def val(t, part, ring=EARLY):
                if mid:
                    held["v"] = v_r[t] = values(j, t, part, ring, held.get("v"))

            def stats1(t):
                if nxt:
                    ln_stats(0, j + 1, t, loaded[j + 1])

            def sc(t, g):
                if mid and t < TILES:
                    scores(t, g, [qn_r[2 * (g % 2)], qn_r[2 * (g % 2) + 1]])

            def key(t):
                if mid and t < TILES:
                    kt[t] = keys_by_token(t, list(k_r.values()))

            def inner(t):
                if mid:
                    y[t] = attend(t, j, v_r[t])

            def upd(t):
                if mid and not ((j + 1) % PER == 0 and t == TILES - 1):
                    update(t, j, kt[t], v_r[t])

            def outer(t, part):
                if mid and t >= 0:
                    if part == 0:
                        held[t] = project_out(t, j, y[t], 0)
                    else:
                        ln_stats(1, j, t, project_out(t, j, y[t], 1, held[t]))

            norm3()
            keys(0)
            stats1(0)
            queries(0)
            stats1(1)
            keys(1)
            chunk(0, 0)
            stats1(2)
            queries(1)
            chunk(0, 1)
            stats1(3)
            den(0)
            keys(2)
            fin(0, 0)
            chunk(0, 2)
            rec(0, 0)
            queries(2)
            fin(0, 1)
            chunk(0, 3)
            rec(0, 1)
            norm1()
            den(1)
            keys(3)
            fin(0, 2)
            rec(1, 0)
            queries(3)
            fin(0, 3)
            rec(1, 1)
            chunk(1, 0)
            den(2)
            val(0, 0)
            val(0, 1)
            chunk(1, 1)
            rec(2, 0)
            val(1, 0)
            val(1, 1)
            fin(1, 0)
            chunk(1, 2)
            rec(2, 1)
            den(3)
            for t in range(TILES):
                bias(0, t)
            val(2, 0)
            val(2, 1)
            fin(1, 1)
            chunk(1, 3, LATE)
            rec(3, 0)
            sc(0, 0)
            rec(3, 1)
            sc(0, 2)
            fin(1, 2)
            f2(j - 2, 2)
            fin(1, 3)
            hidden(0)
            f2(j - 2, 3)
            key(0)
            sc(0, 1)
            val(3, 0, LATE)
            sc(0, 3)
            key(1)
            val(3, 1)
            for t in range(TILES):
                bias(1, t)

            for t in range(TILES):
                inner(t)
                if t < 2:
                    hidden(4 * t + 1)
                if t == 3:
                    norm2()
                sc(t + 1, 0)
                upd(t)
                sc(t + 1, 1)
                outer(t - 1, 0)
                if t == 2:
                    f1(0)
                sc(t + 1, 2)
                if t == 2:
                    f1(1, 2)
                sc(t + 1, 3)
                if t < 2:
                    hidden(4 * t + 2)
                    hidden(*((4 * t + 3, 4 * t + 4) if t == 0 else (4 * t + 3,)))
                outer(t - 1, 1)
                key(t + 2)
                if t == 2:
                    f1(3)
            outer(3, 0)
            f2(j - 1, 0)
            outer(3, 1)
            f2(j - 1, 1)
            t2(0, 1, 2, 3)
        for b in range(NB - SLOTS, NB):
            sp.wait(stored[b])

        block = ctx.enter_context(nc.Block())

        @block.sync
        def _(eng):
            sp.run(eng)

        @block.gpsimd
        def _(eng):
            pool.run(eng)

        @block.scalar
        def _(eng):
            act.run(eng)

        @block.vector
        def _(eng):
            dve.run(eng)

        @block.tensor
        def _(eng):
            pe.run(eng)


_INS = ["L0_attn_x", "L0_attn_w_attn", "L0_attn_w_proj", "L0_ffn_Win", "L0_ffn_bin_", "L0_ffn_W1", "L0_ffn_b1",
        "L0_ffn_W2", "L0_ffn_b2", "L0_ffn_Wout", "L0_ffn_bout"]
_OUTS = [((16, 1024, 512), "float32")]


def kernel(**inputs):
    import numpy as _np
    import concourse.bacc as _bacc
    from concourse import mybir as _mybir
    from concourse.bass_utils import run_bass_kernel_spmd as _run

    nc = _bacc.Bacc("TRN2", target_bir_lowering=False, num_devices=1)
    arrays, args = {}, []
    for name in _INS:
        a = _np.ascontiguousarray(inputs[name])
        arrays[f"in_{name}_dram"] = a
        args.append(nc.dram_tensor(f"in_{name}_dram", a.shape, _mybir.dt.from_np(a.dtype), kind="ExternalInput").ap())
    for i, (shape, dtype) in enumerate(_OUTS):
        dt = _mybir.dt.from_np(_np.dtype(dtype))
        args.append(nc.dram_tensor(f"out_{i}_dram", shape, dt, kind="ExternalOutput").ap())
    macaron_kernel(nc, *args)
    r = _run(nc, [arrays], core_ids=[0])
    return r.results[0]["out_0_dram"]
```

```python
from contextlib import ExitStack

import concourse.bass as bass
from concourse import mybir

F32 = mybir.dt.float32
F32R = mybir.dt.float32r
ALU = mybir.AluOpType
ACT = mybir.ActivationFunctionType

P = 128
TILES = 4
BLK = P * TILES
SLOTS = 5


class Queue:

    def __init__(self, sem):
        self.sem, self.count, self.ops, self.seen = sem, 0, [], {}

    def wait(self, *marks):
        for mark in marks:
            if mark is None:
                continue
            sem, value = mark
            if self.seen.get(id(sem), 0) < value:
                self.seen[id(sem)] = value
                self.ops.append(lambda e, sem=sem, value=value: e.wait_ge(sem, value))

    def put(self, fn):
        self.ops.append(fn)

    def do(self, fn):
        self.count += 1
        sem = self.sem
        self.ops.append(lambda e: fn(e).then_inc(sem, 1))
        return sem, self.count

    def dma(self, fn, sem, total):
        self.ops.append(lambda e: fn(e).then_inc(sem, 16))
        return sem, total

    def run(self, eng):
        for op in self.ops:
            op(eng)


def macaron_kernel(nc, x, w_attn, w_proj, Win, bin_, W1, b1, W2, b2, Wout, bout, out):
    B, T, C = x.shape
    M, INNER = W1.shape
    D = 32
    KC = C // P
    NB = B * T // BLK
    PER = T // BLK
    HB = BLK // 2
    LN_EPS, EPS = 1e-5, 1e-6
    assert C == 512 and M == 64 and INNER == 16 and T % BLK == 0

    xv = x.rearrange("b t c -> (b t) c").rearrange("(k q p) c -> k p q c", q=TILES, p=P)
    ov = out.rearrange("b t c -> (b t) c").rearrange("(k q p) c -> k p q c", q=TILES, p=P)

    ctx = ExitStack()
    with ctx:
        def sb(name, shape, dt=F32):
            return ctx.enter_context(nc.sbuf_tensor(name, shape, dt))

        def sem(name):
            return ctx.enter_context(nc.semaphore(name))

        wa_h, wa_l = sb("wa_h", [P, KC, 3 * C], F32R), sb("wa_l", [P, KC, 3 * C], F32R)
        wp_h, wp_l = sb("wp_h", [P, KC, C], F32R), sb("wp_l", [P, KC, C], F32R)
        win = sb("win", [P, KC, P], F32R)
        wo_h, wo_l = sb("wo_h", [P, C], F32R), sb("wo_l", [P, C], F32R)
        hbout = sb("hbout", [P, C])
        ident, tri, bones = sb("ident", [P, P]), sb("tri", [P, P]), sb("bones", [P, P])
        ones = sb("ones", [1, P])
        w1c, b1c, w2c = sb("w1c", [P, INNER]), sb("b1c", [P, INNER]), sb("w2c", [P, INNER])
        binc, b2c = sb("binc", [P, 1]), sb("b2c", [P, 1])
        mhalf = sb("mhalf", [P, TILES])

        res = [sb(f"res{i}", [P, TILES, C]) for i in range(SLOTS)]
        xhat = [sb(f"xhat{i}", [P, C]) for i in range(4)]
        xh, xl = sb("xh", [P, KC, BLK], F32R), sb("xl", [P, KC, BLK], F32R)
        qT, kT = sb("qT", [P, 4, BLK]), sb("kT", [P, 4, BLK])
        v = sb("v", [P, TILES, C])
        A = sb("A", [P, 4, 4, P])
        ktok = [sb(f"ktok{i}", [P, C]) for i in range(2)]
        S = sb("S", [P, 4, P])
        yh = [sb(f"yh{i}", [P, 4, P], F32R) for i in range(2)]
        yl = [sb(f"yl{i}", [P, 4, P], F32R) for i in range(2)]
        ffs, fft = sb("ffs", [P, 2, HB]), sb("fft", [P, HB])
        ffr = [sb(f"ffr{i}", [P, 2, HB]) for i in range(2)]
        acc = sb("acc", [P, 2, HB])
        gate = sb("gate", [P, 2, 2, HB], F32R)
        z2 = sb("z2", [P, 2, BLK])
        zc = sb("zc", [P, 4])
        st = sb("st", [P, 3, TILES, 6])
        mv = sb("mv", [P, 3, TILES, 2])
        rstd = sb("rstd", [P, 3, TILES])
        nmr = sb("nmr", [P, 3, TILES])
        zh, zl = sb("zh", [P, BLK], F32R), sb("zl", [P, BLK], F32R)
        bones_r = sb("bones_r", [P, P], F32R)

        bank = [ctx.enter_context(nc.psum_tensor(f"bank{i}", [P, 512], F32)) for i in range(8)]

        pe, act, dve, pool = (Queue(sem(n)) for n in ("s_pe", "s_act", "s_dve", "s_pool"))
        sp = Queue(sem("s_sp"))
        s_ld = [sem(f"s_ld{i}") for i in range(SLOTS)]
        s_st = [sem(f"s_st{i}") for i in range(SLOTS)]

        free = [None] * 8
        turn, taken = [0], [0] * 8
        busy = set()

        def take():
            turn[0] += 1
            b = min((b for b in ring[0] if b not in busy), key=lambda b: taken[b])
            taken[b] = turn[0]
            pe.wait(free[b])
            return b

        LATE, EARLY = (5, 6, 7), (5, 6, 7, 0, 1, 2, 3)
        ring = [EARLY]
        NUM = 4

        def f32(ap):
            return ap.bitcast(F32)

        def mm(o, l, r, start, stop, **kw):
            pe.put(lambda e: e.matmul(o, l, r, start=start, stop=stop, **kw))

        def mm_done(o, l, r, start, stop, **kw):
            return pe.do(lambda e: e.matmul(o, l, r, start=start, stop=stop, **kw))

        def split3(o, pairs, first=True, last=True):
            n = 3 * len(pairs)
            i = 0
            for lh, ll, rh, rl in pairs:
                for l, r in ((lh, rh), (lh, rl), (ll, rh)):
                    i += 1
                    f = mm if i < n else mm_done
                    done = f(o, l, r, first and i == 1, last and i == n)
            return done

        s_c = {}

        def load_const(name, dst, src):
            s_c[name] = sem(f"s_{name}")
            return sp.dma(lambda e: e.dma_start(dst, src), s_c[name], 16)

        loaded = {}

        def load(b):
            s = b % SLOTS
            if b >= SLOTS:
                sp.wait(stored[b - SLOTS])
            loaded[b] = sp.dma(lambda e: e.dma_start(res[s][:, :, :], xv[b]), s_ld[s], 16 * (b // SLOTS + 1))

        stored = {}

        def store(b, done):
            s = b % SLOTS
            sp.wait(done)
            stored[b] = sp.dma(lambda e: e.dma_start(ov[b], res[s][:, :, :]), s_st[s], 16 * (b // SLOTS + 1))

        win_v = Win.rearrange("(k p) m -> p k m", p=P)
        win_st = ffr[0][:, 0, :].rearrange("p (k m) -> p k m", k=KC)
        wo_st = z2[:, 0, :]
        load(0)
        l_win = load_const("win", win_st, win_v)
        l_wo0 = load_const("wo0", wo_st[0:M, :], Wout)
        l_wo1 = load_const("wo1", wo_st[M:P, :], Wout)
        load(1)
        l_small = []
        for name, dst, src in (("w1", w1c, W1), ("b1", b1c, b1), ("w2", w2c, W2)):
            for h in range(2):
                l_small.append(load_const(f"{name}{h}", dst[M * h:M * h + M, :], src))
        for h in range(2):
            l_small.append(load_const(f"bin{h}", binc[M * h:M * h + M, :], bin_.rearrange("(m a) -> m a", a=1)))
            l_small.append(load_const(f"b2{h}", b2c[M * h:M * h + M, :], b2.rearrange("(m a) -> m a", a=1)))
        l_bout = load_const("bout", z2[0:1, 1, :], bout.rearrange("(a n) -> a n", a=1))
        wa_v = w_attn.rearrange("(k p) n -> p k n", p=P)
        wa_st = [qT, kT, v]
        l_wa = {n: load_const(f"wa{n}", wa_st[n][:, :, :], wa_v[:, :, n * C:n * C + C]) for n in (1, 0, 2)}
        wp_st = A[:, :, :, :].rearrange("p h g n -> p h (g n)")
        l_wp = load_const("wp", wp_st, w_proj.rearrange("(k p) n -> p k n", p=P))
        load(2)

        z_id = pool.do(lambda e: e.memset(ident[:, :], 0.0))
        z_tri = pool.do(lambda e: e.memset(tri[:, :], 1.0))
        z_bones = pool.do(lambda e: e.memset(bones[:, :], 0.0))
        z_S = pool.do(lambda e: e.memset(S[:, :, :], 0.0))
        c_ones = pool.do(lambda e: e.memset(ones[:, :], 1.0))
        c_half = pool.do(lambda e: e.memset(mhalf[:, :], -0.5))
        pool.wait(z_id)
        c_ident = pool.do(lambda e: e.affine_select(out=ident[:, :], in_=ident[:, :], compare_op=ALU.not_equal, fill=1.0,
                                                    base=0, pattern=[[-1, P]], channel_multiplier=1))
        pool.wait(z_tri)
        c_tri = pool.do(lambda e: e.affine_select(out=tri[:, :], in_=tri[:, :], compare_op=ALU.is_ge, fill=0.0,
                                                  base=0, pattern=[[1, P]], channel_multiplier=-1))
        pool.wait(z_bones)
        pool.wait(c_tri)
        for h in range(4):
            if h:
                pool.wait(c_bones)
            c_bones = pool.do(lambda e, h=h: e.memset(bones[D * h:D * h + D, D * h:D * h + D], 1.0))

        act.wait(c_bones)
        c_bones = act.do(lambda e: e.activation(bones_r[:, :], bones[:, :], ACT.Copy))

        def split_weight(eng, src, hi, lo, *ready):
            act.wait(*ready)
            h = act.do(lambda e: e.activation(hi, src, ACT.Copy))
            eng.wait(h, *ready)
            return eng.do(lambda e: e.tensor_tensor(lo, src, f32(hi), ALU.subtract))

        w_in = split_weight(dve, win_st, win[:, :, 0:M], win[:, :, M:P], l_win)
        w_out = split_weight(dve, wo_st, wo_h[:, :], wo_l[:, :], l_wo0, l_wo1)
        w_a = {}

        pe.wait(l_bout, c_ones)
        b = take()
        m_bout = mm_done(bank[b][:, :], ones[0:1, :], z2[0:1, 1, :], True, True)
        act.wait(m_bout)
        c_bout = act.do(lambda e, b=b: e.activation(hbout[:, :], bank[b][:, :], ACT.Copy, scale=0.5))
        free[b] = c_bout

        stats_done, norm_last = {}, [None] * 3
        xhat_free = [None] * 4
        xturn = [0]
        xhat_ready = {}

        def ln_stats(n, b, t, ready):
            r = res[b % SLOTS]
            dve.wait(ready, norm_last[n])
            s = dve.do(lambda e: e.bn_stats(st[:, n, t, :], r[:, t, :]))
            dve.wait(s)
            aggr = dve.do(lambda e: e.bn_aggr(mv[:, n, t, :], st[:, n, t, :]))
            if t == TILES - 1:
                pool.wait(aggr, norm_last[n], c_half)
                ve = pool.do(lambda e: e.tensor_scalar(nmr[:, n, :], mv[:, n, :, 1], LN_EPS, None, ALU.add))
                pool.wait(ve)
                pw = pool.do(lambda e: e.tensor_tensor(rstd[:, n, :], nmr[:, n, :], mhalf[:, :], ALU.pow))
                dve.wait(pw, aggr)
                stats_done[n, b] = dve.do(lambda e: e.scalar_tensor_tensor(
                    nmr[:, n, :], mv[:, n, :, 0], -1.0, rstd[:, n, :], ALU.mult, ALU.mult))

        def normalise(n, b, t):
            i = xturn[0] % 4
            xturn[0] += 1
            r = res[b % SLOTS]
            act.wait(stats_done[n, b], xhat_free[i])
            done = act.do(lambda e: e.activation(xhat[i][:, :], r[:, t, :], ACT.Identity,
                                                 bias=nmr[:, n, t:t + 1], scale=rstd[:, n, t:t + 1]))
            xhat_ready[n, b, t] = (i, done)
            norm_last[n] = done

        xT_free = [None]
        xT_ready = {}

        def to_channels(n, b, t):
            i, ready = xhat_ready.pop((n, b, t))
            k = take()
            pe.wait(ready, c_ident)
            for c in range(KC):
                f = pe.do if c == KC - 1 else pe.put
                done = f(lambda e, c=c: e.transpose(bank[k][:, c * P:c * P + P], xhat[i][:, c * P:c * P + P], ident[:, :]))
            xhat_free[i] = done
            src = bank[k][:, :].rearrange("p (c t) -> p c t", c=KC)
            act.wait(done, xT_free[0])
            h = act.do(lambda e: e.activation(xh[:, :, t * P:t * P + P], src, ACT.Copy))
            dve.wait(h, xT_free[0])
            lo = dve.do(lambda e: e.tensor_tensor(xl[:, :, t * P:t * P + P], src, f32(xh[:, :, t * P:t * P + P]), ALU.subtract))
            free[k] = lo
            xT_ready[n, b] = (h, lo)

        def add_bias(b, t, after):
            r = res[b % SLOTS]
            pool.wait(after, c_bout)
            return pool.do(lambda e: e.tensor_tensor(r[:, t, :], r[:, t, :], hbout[:, :], ALU.add))

        ff = {"g_done": None, "t_free": None, "r_free": [None, None], "s_free": None, "acc_done": None, "g_free": None}

        def chunk_to_channels(n, b, c):
            k, o = take(), c % 2
            pe.wait(c_ident)
            for t in range(TILES):
                i, ready = xhat_ready[n, b, t]
                pe.wait(ready)
                f = pe.do if t == TILES - 1 else pe.put
                done = f(lambda e, t=t, i=i: e.transpose(bank[k][:, t * P:t * P + P], xhat[i][:, c * P:c * P + P], ident[:, :]))
            if c == KC - 1:
                for t in range(TILES):
                    xhat_free[xhat_ready.pop((n, b, t))[0]] = done
            src = bank[k][:, :].rearrange("p (g t) -> p g t", g=4)
            act.wait(done, at["y_free"][o])
            h = act.do(lambda e: e.activation(yh[o][:, :, :], src, ACT.Copy))
            dve.wait(h, at["y_free"][o])
            free[k] = dve.do(lambda e: e.tensor_tensor(yl[o][:, :, :], src, f32(yh[o][:, :, :]), ALU.subtract))
            ff["chunk", c] = (h, free[k])

        def ff_in(half, c):
            k, o = NUM, c % 2
            if c == 0:
                pe.wait(free[k])
            pe.wait(w_in, *ff["chunk", c])
            mm(bank[k][:, :], win[:, c, :], yh[o][:, :, :].rearrange("p g t -> p (g t)"), c == 0, False)
            done = mm_done(bank[k][:, :], win[:, c, :], yl[o][:, :, :].rearrange("p g t -> p (g t)"), False, c == KC - 1)
            at["y_free"][o] = done
            if c < KC - 1:
                return
            act.wait(done, ff["t_free"], *l_small)
            for s in range(2):
                here, there = slice(M * s, M * s + M), slice(M - M * s, 2 * M - M * s)
                w = slice(HB * s, HB * s + HB)
                a = act.do(lambda e, here=here, there=there, w=w: e.activation(
                    fft[here, :], bank[k][there, w], ACT.Identity, bias=binc[there, 0:1]))
            dve.wait(a, ff["s_free"])
            for s in range(2):
                here, w = slice(M * s, M * s + M), slice(HB * s, HB * s + HB)
                d = dve.do(lambda e, here=here, w=w: e.tensor_tensor(ffs[here, half, :], bank[k][here, w], fft[here, :], ALU.add))
            free[k] = ff["t_free"] = d
            return d

        def ff_hidden(i, lo, hi, ready):
            r = ffr[i % 2]
            act.wait(ready, ff["r_free"][i % 2])
            a = act.do(lambda e: e.activation(r[:, lo:hi, :], ffs[:, lo:hi, :], ACT.Relu,
                                              bias=b1c[:, i:i + 1], scale=w1c[:, i:i + 1]))
            ff["s_free"] = a
            dve.wait(a, ff["acc_done"], *l_small)
            if i == 0:
                dve.wait(ff["g_done"])
                d = dve.do(lambda e: e.tensor_scalar(acc[:, lo:hi, :], r[:, lo:hi, :], w2c[:, 0:1], b2c[:, 0:1],
                                                     ALU.mult, ALU.add))
            else:
                d = dve.do(lambda e: e.scalar_tensor_tensor(acc[:, lo:hi, :], r[:, lo:hi, :], w2c[:, i:i + 1],
                                                            acc[:, lo:hi, :], ALU.mult, ALU.add))
            ff["acc_done"] = ff["r_free"][i % 2] = d

        def ff_gate(lo, hi):
            for s in range(2):
                here, there = slice(M * s, M * s + M), slice(M - M * s, 2 * M - M * s)
                act.wait(ff["acc_done"], ff["g_free"])
                h = act.do(lambda e, s=s, here=here: e.activation(gate[here, lo:hi, s, :], acc[here, lo:hi, :], ACT.Copy))
                dve.wait(h, ff["acc_done"], ff["g_free"])
                ff["g_done"] = dve.do(lambda e, s=s, here=here, there=there: e.tensor_tensor(
                    gate[there, lo:hi, s, :], acc[here, lo:hi, :], f32(gate[here, lo:hi, s, :]), ALU.subtract))

        def ff_out(b, t, half, biased):
            k = take()
            pe.wait(ff["g_done"], w_out)
            s, w = t // 2, slice(t % 2 * P, t % 2 * P + P)
            mm(bank[k][:, :], gate[:, half, s, w], wo_h[:, :], True, False)
            done = mm_done(bank[k][:, :], gate[:, half, s, w], wo_l[:, :], False, True)
            ff["g_free"] = done
            r = res[b % SLOTS]
            dve.wait(done, biased)
            free[k] = dve.do(lambda e: e.scalar_tensor_tensor(r[:, t, :], bank[k][:, :], 0.5, r[:, t, :], ALU.mult, ALU.add))
            return free[k]

        at = {"kq_free": None, "v_free": [None] * TILES, "z_free": [None, None],
              "rd_free": [None, None], "zc": [None] * 4, "S": None, "S_free": None, "kt_free": [None, None],
              "A_free": None, "zs_free": None, "y_free": [None, None]}

        def project(g, which, b):
            dst = (qT, kT)[which]
            k = take()
            col = which * C + g * P
            pe.wait(w_a[which], *xT_ready[2, b])
            done = split3(bank[k][:, :], [(wa_h[:, c, col:col + P], wa_l[:, c, col:col + P], xh[:, c, :], xl[:, c, :])
                                          for c in range(KC)])
            xT_free[0] = done
            act.wait(done, w_a[which], at["kq_free"])
            n = act.do(lambda e: e.activation(dst[:, g, :], bank[k][:, :], ACT.Relu, scale=-1.0))
            act.wait(n)
            a = act.do(lambda e: e.activation(dst[:, g, :], dst[:, g, :], ACT.Exp, scale=-1.0))
            dve.wait(a)
            free[k] = dve.do(lambda e: e.scalar_tensor_tensor(dst[:, g, :], bank[k][:, :], 0.0, dst[:, g, :], ALU.max, ALU.add))
            return free[k]

        def key_sums(g, b, k_ready, q_ready):
            z = z2[:, g % 2, :]
            first = b % PER == 0
            init = 0.0 if first else zc[:, g:g + 1]
            dve.wait(k_ready, at["rd_free"][g % 2], w_out, m_bout, None if first else at["zc"][g])
            s = dve.do(lambda e: e.tensor_tensor_scan(z, kT[:, g, :], kT[:, g, :], init, ALU.add, ALU.bypass))
            pool.wait(s, q_ready)
            at["zc"][g] = pool.do(lambda e: e.tensor_copy(zc[:, g:g + 1], z[:, BLK - 1:BLK]))
            pool.wait(at["zc"][g])
            return pool.do(lambda e: e.tensor_tensor(z, qT[:, g, :], z, ALU.mult))

        def split_z(g, z_ready):
            z = z2[:, g % 2, :]
            act.wait(z_ready, at["zs_free"])
            h = act.do(lambda e: e.activation(zh[:, :], z, ACT.Copy))
            pool.wait(h, at["zs_free"])
            at["z_free"][g % 2] = pool.do(lambda e: e.tensor_tensor(zl[:, :], z, f32(zh[:, :]), ALU.subtract))
            return at["z_free"][g % 2]

        def denominator(g, z_ready):
            rd = z2[:, g % 2, :]
            k = take()
            pe.wait(z_ready, c_bones)
            mm(bank[k][:, :], bones_r[:, :], zh[:, :], True, False)
            done = mm_done(bank[k][:, :], bones_r[:, :], zl[:, :], False, True)
            at["zs_free"] = done
            act.wait(done, at["z_free"][g % 2])
            a = act.do(lambda e: e.activation(rd, bank[k][:, :], ACT.Identity, bias=EPS))
            free[k] = a
            return a

        def normalise_q(g, half, ready):
            w = slice(half * (BLK // 2), (half + 1) * (BLK // 2))
            rd = z2[:, g % 2, w]
            dve.wait(ready)
            r = dve.do(lambda e: e.reciprocal(rd, rd))
            pool.wait(r)
            at["rd_free"][g % 2] = pool.do(lambda e: e.tensor_tensor(qT[:, g, w], qT[:, g, w], rd, ALU.mult))
            return at["rd_free"][g % 2]

        def values(b, t, part, k=None):
            if part == 0:
                k = take()
            w = slice(t * P, t * P + P)
            pe.wait(w_a[2])
            done = split3(bank[k][:, :], [(xh[:, c, w], xl[:, c, w], wa_h[:, c, 2 * C:], wa_l[:, c, 2 * C:])
                                          for c in (2 * part, 2 * part + 1)], part == 0, part == 1)
            if part == 0:
                busy.add(k)
                return k
            busy.remove(k)
            xT_free[0] = done
            act.wait(done, at["v_free"][t], w_a[2])
            free[k] = act.do(lambda e: e.activation(v[:, t, :], bank[k][:, :], ACT.Copy))
            return free[k]

        def keys_by_token(t, k_ready):
            k = take()
            pe.wait(*k_ready, c_ident)
            w = slice(t * P, t * P + P)
            for g in range(4):
                f = pe.do if g == 3 else pe.put
                done = f(lambda e, g=g: e.transpose(bank[k][:, g * P:g * P + P], kT[:, g, w], ident[:, :]))
            at["kq_free"] = done
            act.wait(done, at["kt_free"][t % 2])
            free[k] = act.do(lambda e: e.activation(ktok[t % 2][:, :], bank[k][:, :], ACT.Copy))
            return free[k]

        def scores(t, part, qn_ready):
            w = slice(t * P, t * P + P)
            heads = (0, 1) if part < 2 else (2, 3)
            if part % 2 == 0:
                assert not busy & set(heads)
                busy.update(heads)
                for h in heads:
                    taken[h] = turn[0]
                for h in heads:
                    pe.wait(free[h])
            pe.wait(*qn_ready)
            done = {}
            for g in ((0, 1), (2, 3))[part % 2]:
                for h in heads:
                    d = slice(D * h, D * h + D)
                    f = mm_done if g == 3 else mm
                    done[h] = f(bank[h][:, g * P:g * P + P], kT[d, g, w], qT[d, g, w], True, True)
            if part % 2 == 0:
                return
            at["kq_free"] = done[heads[1]]
            return done

        def causal(h, ready):
            mask = tri[:, :].unsqueeze(1).to_broadcast([P, 4, P])
            src = bank[h][:, :].rearrange("p (g i) -> p g i", g=4)
            if h in (0, 2):
                act.wait(at["A_free"], w_p, ready)
                free[h] = act.do(lambda e: e.activation(A[:, h, :, :], src, ACT.Copy))
                pool.wait(c_tri, free[h])
                at["A", h] = pool.do(lambda e: e.tensor_tensor(A[:, h, :, :], A[:, h, :, :], mask, ALU.mult))
            else:
                dve.wait(c_tri, at["A_free"], w_p, ready)
                at["A", h] = free[h] = dve.do(lambda e: e.tensor_tensor(A[:, h, :, :], src, mask, ALU.mult))
            busy.remove(h)

        def attend(t, b, v_ready):
            w = slice(t * P, t * P + P)
            first = b % PER == 0 and t == 0
            pe.wait(free[NUM])
            num = bank[NUM]
            if not first:
                pe.wait(at["S"])
                for g in range(4):
                    f = mm_done if g == 3 else mm
                    done = f(num[:, g * P:g * P + P], S[:, g, :], qT[:, g, w], g == 0, False, skip_group_check=True)
                at["S_free"] = at["kq_free"] = done
            pe.wait(*(at["A", h] for h in range(4)), v_ready)
            for g in range(4):
                for h in range(4):
                    d = slice(D * h, D * h + D)
                    f = mm_done if (g, h) == (3, 3) else mm
                    done = f(num[d, g * P:g * P + P], v[:, t, (4 * g + h) * D:(4 * g + h + 1) * D], A[:, h, g, :],
                             first and g == 0, True, skip_group_check=True)
            at["A_free"] = at["v_free"][t] = done
            return done

        def split_y(t, ready):
            src = bank[NUM][:, :].rearrange("p (g i) -> p g i", g=4)
            o = t % 2
            act.wait(ready, at["y_free"][o])
            a = act.do(lambda e: e.activation(yh[o][:, :, :], src, ACT.Copy))
            dve.wait(a, at["y_free"][o])
            free[NUM] = dve.do(lambda e: e.tensor_tensor(yl[o][:, :, :], src, f32(yh[o][:, :, :]), ALU.subtract))
            return a, free[NUM]

        def update(t, b, kt_ready, v_ready):
            k = take()
            pe.wait(kt_ready, v_ready)
            for g in range(4):
                for h in range(4):
                    d, n = slice(D * h, D * h + D), slice(g * P + D * h, g * P + D * h + D)
                    f = mm_done if (g, h) == (3, 3) else mm
                    done = f(bank[k][d, g * D:g * D + D], ktok[t % 2][:, n], v[:, t, n], True, True)
            at["kt_free"][t % 2] = at["v_free"][t] = done
            src = bank[k][:, 0:P].rearrange("p (g n) -> p g n", g=4)
            first = b % PER == 0 and t == 0
            dve.wait(done, at["S_free"], at["S"], z_S)
            for h in range(4):
                d = slice(D * h, D * h + D)
                if first:
                    s = dve.do(lambda e, d=d: e.tensor_copy(S[d, :, d], src[d, :, :]))
                else:
                    s = dve.do(lambda e, d=d: e.tensor_tensor(S[d, :, d], src[d, :, :], S[d, :, d], ALU.add))
            at["S"] = free[k] = s

        def project_out(t, b, y_ready, part, k=None):
            if part == 0:
                k = take()
            o = t % 2
            pe.wait(*y_ready, w_p)
            done = split3(bank[k][:, :], [(yh[o][:, g, :], yl[o][:, g, :], wp_h[:, g, :], wp_l[:, g, :])
                                          for g in (2 * part, 2 * part + 1)], part == 0, part == 1)
            if part == 0:
                busy.add(k)
                return k
            busy.remove(k)
            at["y_free"][o] = done
            r = res[b % SLOTS]
            dve.wait(done)
            free[k] = dve.do(lambda e: e.tensor_tensor(r[:, t, :], bank[k][:, :], r[:, t, :], ALU.add))
            return free[k]

        biased, normed = {}, {}
        load(3)
        load(4)
        w_p = None

        def split_qkv(n):
            w_a[n] = split_weight(pool, wa_st[n][:, :, :], wa_h[:, :, n * C:n * C + C], wa_l[:, :, n * C:n * C + C], l_wa[n])

        for t in range(TILES):
            ln_stats(0, 0, t, loaded[0])
        for b in range(2):
            for t in range(TILES):
                normalise(0, b, t)
            last_norm = norm_last[0]
            if b == 0:
                for t in range(TILES):
                    ln_stats(0, 1, t, loaded[1])
            for c in range(KC):
                chunk_to_channels(0, b, c)
                if c:
                    ff_in(b, c - 1)
            ffs_ready = ff_in(b, KC - 1)
            for t in range(TILES):
                biased[b] = add_bias(b, t, last_norm)
        split_qkv(1)
        for i in range(INNER):
            ff_hidden(i, 0, 2, ffs_ready)
        ff_gate(0, 2)
        split_qkv(0)
        for b in range(2):
            for t in range(TILES):
                ln_stats(2, b, t, ff_out(b, t, b, biased[b]))
            if b == 0:
                for t in range(TILES):
                    normalise(2, 0, t)
                for t in range(TILES):
                    to_channels(2, 0, t)
                split_qkv(2)
        w_p = split_weight(pool, wp_st, wp_h[:, :, :], wp_l[:, :, :], l_wp)

        for j in range(NB + 2):
            mid = j < NB
            last = 0 <= j - 1 < NB
            pre = j + 2 < NB
            nxt = j + 1 < NB
            k_r, q_r, z_r, d_r, qn_r, v_r, kt, y, held, ffs_ready = {}, {}, {}, {}, {}, {}, {}, {}, {}, []
            lo, hi = (0 if last else 1), (2 if pre else 1)
            ring[0] = EARLY

            def chunk(half, c):
                if half == 0 and last:
                    chunk_to_channels(1, j - 1, c)
                if half == 1 and pre:
                    chunk_to_channels(0, j + 2, c)

            def fin(half, c):
                if (pre if half else last):
                    done = ff_in(half, c)
                    if c == KC - 1:
                        ffs_ready.append(done)

            def norm3(t):
                if last:
                    normalise(1, j - 1, t)
                    normed[j - 1] = norm_last[1]

            def norm1(t):
                if pre:
                    normalise(0, j + 2, t)
                    normed[j + 2] = norm_last[0]

            def bias(half, t):
                if (pre if half else last):
                    b = j + 2 if half else j - 1
                    biased[b] = add_bias(b, t, normed[b])

            def norm2(t):
                if nxt:
                    normalise(2, j + 1, t)

            def f1(*tiles):
                if pre:
                    for t in tiles:
                        r = ff_out(j + 2, t, 1, biased[j + 2])
                        ln_stats(2, j + 2, t, r)

            def f2(b, *tiles):
                if 0 <= b < NB:
                    for t in tiles:
                        r = ff_out(b, t, 0, biased[b])
                        if t == TILES - 1:
                            store(b, r)
                            if b + SLOTS < NB:
                                load(b + SLOTS)

            def t2(*tiles):
                if nxt:
                    for t in tiles:
                        to_channels(2, j + 1, t)

            def hidden(i):
                if last or pre:
                    ff_hidden(i, lo, hi, ffs_ready[-1])

            def gates():
                if last or pre:
                    ff_gate(lo, hi)

            def keys(g):
                if mid:
                    k_r[g] = project(g, 1, j)

            def queries(g):
                if mid:
                    q_r[g] = project(g, 0, j)

            def zsum(g):
                if mid:
                    z_r[g] = key_sums(g, j, k_r[g], q_r[g])

            def zsplit(g):
                if mid:
                    z_r[g] = split_z(g, z_r[g])

            def den(g):
                if mid:
                    d_r[g] = denominator(g, z_r[g])

            def rec(g, half):
                if mid:
                    qn_r[g] = normalise_q(g, half, d_r[g])

            def val(t, part):
                if mid:
                    held["v", t] = v_r[t] = values(j, t, part, held.get(("v", t)))

            def stats1(t):
                if pre:
                    ln_stats(0, j + 2, t, loaded[j + 2])

            def sc(t, part):
                if mid:
                    ring[0] = LATE
                    held["s", t, part] = scores(t, part, [qn_r[2 * (part % 2)], qn_r[2 * (part % 2) + 1]])

            def mask(t, h):
                if mid:
                    causal(h, held["s", t, 1 + h // 2 * 2][h])

            def key(t):
                if mid:
                    kt[t] = keys_by_token(t, list(k_r.values()))

            def inner(t):
                if mid:
                    held["n", t] = attend(t, j, v_r[t])

            def ysplit(t):
                if mid:
                    y[t] = split_y(t, held["n", t])

            def upd(t):
                if mid and not ((j + 1) % PER == 0 and t == TILES - 1):
                    update(t, j, kt[t], v_r[t])

            def outer(t, part):
                if mid:
                    if part == 0:
                        held[t] = project_out(t, j, y[t], 0)
                    else:
                        ln_stats(1, j, t, project_out(t, j, y[t], 1, held[t]))

            stats1(0)
            norm3(0)
            stats1(1)
            norm3(1)
            norm3(2)
            queries(0)
            queries(1)
            norm3(3)
            keys(0)
            stats1(2)
            zsum(0)
            keys(1)
            chunk(0, 0)
            stats1(3)
            zsplit(0)
            chunk(0, 1)
            keys(2)
            zsum(1)
            queries(3)
            fin(0, 0)
            chunk(0, 2)
            fin(0, 1)
            den(0)
            zsplit(1)
            rec(0, 0)
            chunk(0, 3)
            norm1(0)
            rec(0, 1)
            queries(2)
            den(1)
            rec(1, 0)
            zsum(2)
            fin(0, 2)
            rec(1, 1)
            norm1(1)
            fin(0, 3)
            norm1(2)
            norm1(3)
            keys(3)
            zsplit(2)
            zsum(3)
            val(0, 0)
            chunk(1, 0)
            chunk(1, 1)
            val(0, 1)
            val(1, 0)
            den(2)
            key(0)
            zsplit(3)
            val(1, 1)
            rec(2, 0)
            fin(1, 0)
            fin(1, 1)
            rec(2, 1)
            chunk(1, 2)
            chunk(1, 3)
            sc(0, 2)
            key(1)
            den(3)
            rec(3, 0)
            rec(3, 1)
            fin(1, 2)
            fin(1, 3)
            val(2, 0)
            val(3, 0)
            f2(j - 2, 2)
            norm2(0)
            norm2(1)
            hidden(0)
            hidden(1)
            hidden(2)
            sc(0, 0)
            val(2, 1)
            sc(0, 3)
            mask(0, 2)
            mask(0, 3)
            sc(0, 1)
            norm2(2)
            mask(0, 0)
            val(3, 1)
            mask(0, 1)
            hidden(3)
            t2(0)
            sc(1, 2)
            sc(1, 0)
            hidden(4)
            hidden(5)
            t2(1)
            bias(1, 0)
            inner(0)
            upd(0)
            hidden(6)
            sc(1, 1)
            mask(1, 1)
            mask(1, 0)
            key(2)
            sc(1, 3)
            hidden(7)
            ysplit(0)
            mask(1, 3)
            f2(j - 2, 3)
            mask(1, 2)
            t2(2)
            sc(2, 0)
            sc(2, 1)
            hidden(8)
            inner(1)
            upd(1)
            mask(2, 1)
            sc(2, 2)
            outer(0, 0)
            sc(2, 3)
            mask(2, 0)
            sc(3, 0)
            sc(3, 1)
            bias(0, 0)
            hidden(9)
            mask(2, 3)
            norm2(3)
            ysplit(1)
            hidden(10)
            hidden(11)
            outer(0, 1)
            mask(2, 2)
            sc(3, 2)
            inner(2)
            hidden(12)
            hidden(13)
            mask(3, 1)
            hidden(14)
            hidden(15)
            upd(2)
            sc(3, 3)
            mask(3, 2)
            ysplit(2)
            mask(3, 0)
            outer(1, 0)
            outer(1, 1)
            bias(0, 1)
            bias(0, 2)
            mask(3, 3)
            bias(1, 1)
            gates()
            t2(3)
            outer(2, 0)
            outer(2, 1)
            bias(0, 3)
            inner(3)
            ysplit(3)
            key(3)
            f2(j - 1, 0)
            f2(j - 1, 1)
            f1(0)
            upd(3)
            f1(1)
            bias(1, 2)
            bias(1, 3)
            outer(3, 0)
            outer(3, 1)
            f1(2)
            f1(3)
        for b in range(NB - SLOTS, NB):
            sp.wait(stored[b])

        block = ctx.enter_context(nc.Block())

        @block.sync
        def _(eng):
            sp.run(eng)

        @block.gpsimd
        def _(eng):
            pool.run(eng)

        @block.scalar
        def _(eng):
            act.run(eng)

        @block.vector
        def _(eng):
            dve.run(eng)

        @block.tensor
        def _(eng):
            pe.run(eng)


_INS = ["L0_attn_x", "L0_attn_w_attn", "L0_attn_w_proj", "L0_ffn_Win", "L0_ffn_bin_", "L0_ffn_W1", "L0_ffn_b1",
        "L0_ffn_W2", "L0_ffn_b2", "L0_ffn_Wout", "L0_ffn_bout"]
_OUTS = [((16, 1024, 512), "float32")]


def kernel(**inputs):
    import numpy as _np
    import concourse.bacc as _bacc
    from concourse import mybir as _mybir
    from concourse.bass_utils import run_bass_kernel_spmd as _run

    nc = _bacc.Bacc("TRN2", target_bir_lowering=False, num_devices=1)
    arrays, args = {}, []
    for name in _INS:
        a = _np.ascontiguousarray(inputs[name])
        arrays[f"in_{name}_dram"] = a
        args.append(nc.dram_tensor(f"in_{name}_dram", a.shape, _mybir.dt.from_np(a.dtype), kind="ExternalInput").ap())
    for i, (shape, dtype) in enumerate(_OUTS):
        dt = _mybir.dt.from_np(_np.dtype(dtype))
        args.append(nc.dram_tensor(f"out_{i}_dram", shape, dt, kind="ExternalOutput").ap())
    macaron_kernel(nc, *args)
    r = _run(nc, [arrays], core_ids=[0])
    return r.results[0]["out_0_dram"]
```
